# Optimizing a Trainium2 kernel written in Bass

```python
import numpy as np
import jax
import jax.numpy as jnp

def _softmax(x, axis=-1):
    return jax.nn.softmax(x, axis=axis)

def _gelu(x):
    return jax.nn.gelu(x, approximate=True)

def _silu(x):
    return jax.nn.silu(x)

def _sigmoid(x):
    return jax.nn.sigmoid(x)

def _layernorm(x, axis=-1, eps=1e-05):
    m = jnp.mean(x, axis=axis, keepdims=True)
    v = jnp.var(x, axis=axis, keepdims=True)
    return (x - m) / jnp.sqrt(v + eps)

def _scatter_add(tgt, idx, src, axis=0):
    return tgt.at[idx].add(src)

def _segment_sum(src, seg, n):
    return jax.ops.segment_sum(src, seg, n)
kernel_name = 'mk_gnn_preln_d4_gnn_r8_732dec'

def setup_inputs(seed: int=0):
    np.random.seed(seed)
    _w = jnp.asarray

    def _rec_inputs():
        import jax
        import jax.numpy as jnp
        _gk = jax.random.key(seed)
        x = -0.0005121 + 1.001 * jax.random.normal(jax.random.fold_in(_gk, 1), (12500, 32), jnp.float32)
        src = jax.random.randint(jax.random.fold_in(_gk, 2), (200000,), 0, 12500, jnp.int32)
        dst = jnp.minimum((12500 * jax.random.uniform(jax.random.fold_in(_gk, 3), (200000,)) ** 2.0).astype(jnp.int32), 99999)
        _o = jnp.argsort(dst, stable=True)
        src = src[_o]
        dst = dst[_o]
        edge_attr_3 = 0.000549083 + 1.00031 * jax.random.normal(jax.random.fold_in(_gk, 11), (200000, 3), jnp.float32)
        edge_attr_32 = 0.000216709 + 1.00012 * jax.random.normal(jax.random.fold_in(_gk, 12), (200000, 32), jnp.float32)
        edge_attr_4 = 0.000714719 + 1.00021 * jax.random.normal(jax.random.fold_in(_gk, 13), (200000, 4), jnp.float32)
        edge_attr_5 = -0.000325185 + 1.00005 * jax.random.normal(jax.random.fold_in(_gk, 14), (200000, 5), jnp.float32)
        edge_weight1 = 0.000452788 + 0.999756 * jax.random.normal(jax.random.fold_in(_gk, 16), (200000, 1), jnp.float32)
        return (x, src, dst, edge_attr_3, edge_attr_32, edge_attr_4, edge_attr_5, edge_weight1)
    x, src, dst, edge_attr_3, edge_attr_32, edge_attr_4, edge_attr_5, edge_weight1 = _rec_inputs()

    def _L0_gnn_setup():
        import jax, jax.numpy as jnp
        import numpy as np
        N_NODES = 12500
        N_EDGES = 200000
        LATENT_DIM = 32
        NUM_LAYERS = 3
        key = jax.random.key(seed)
        k_x, k_e = jax.random.split(key)
        x = jax.random.normal(k_x, (N_NODES, LATENT_DIM), dtype=jnp.float32)
        edge_index = jax.random.randint(k_e, (2, N_EDGES), 0, N_NODES, dtype=jnp.int64)
        return {'x': x, 'edge_index': edge_index, 'num_layers': NUM_LAYERS}
    _L0_gnn_all = _L0_gnn_setup()
    _L0_gnn_in = {k: v for k, v in _L0_gnn_all.items() if k in ()}
    del _L0_gnn_all

    def _L1_gnn_setup():
        import jax, jax.numpy as jnp
        import numpy as np
        import math
        M = 8
        COMBOS = [(0, 0, 0), (0, 1, 1), (1, 0, 1), (1, 1, 0), (1, 1, 1), (2, 1, 1)]

        def _cg_coeff(j1, m1, j2, m2, j3, m3):
            if m3 != m1 + m2:
                return 0.0
            f = math.factorial
            vmin = max(0, j2 - j3 - m1, j1 + m2 - j3)
            vmax = min(j1 + j2 - j3, j1 - m1, j2 + m2)
            pref = (2 * j3 + 1) * f(j3 + j1 - j2) * f(j3 - j1 + j2) * f(j1 + j2 - j3) / f(j1 + j2 + j3 + 1)
            pref *= f(j3 + m3) * f(j3 - m3) * f(j1 - m1) * f(j1 + m1) * f(j2 - m2) * f(j2 + m2)
            s = 0.0
            for v in range(vmin, vmax + 1):
                s += (-1) ** v / (f(v) * f(j1 + j2 - j3 - v) * f(j1 - m1 - v) * f(j2 + m2 - v) * f(j3 - j2 + m1 + v) * f(j3 - j1 - m2 + v))
            return math.sqrt(pref) * s

        def _su2_cg(l1, l2, l3):
            C = np.zeros((2 * l1 + 1, 2 * l2 + 1, 2 * l3 + 1), dtype=np.complex128)
            for m1 in range(-l1, l1 + 1):
                for m2 in range(-l2, l2 + 1):
                    m3 = m1 + m2
                    if -l3 <= m3 <= l3:
                        C[m1 + l1, m2 + l2, m3 + l3] = _cg_coeff(l1, m1, l2, m2, l3, m3)
            return C

        def _qmat(l):
            q = np.zeros((2 * l + 1, 2 * l + 1), dtype=np.complex128)
            for m in range(-l, 0):
                q[l + m, l + abs(m)] = 1 / np.sqrt(2)
                q[l + m, l - abs(m)] = -1j / np.sqrt(2)
            q[l, l] = 1.0
            for m in range(1, l + 1):
                q[l + m, l + abs(m)] = (-1) ** m / np.sqrt(2)
                q[l + m, l - abs(m)] = 1j * (-1) ** m / np.sqrt(2)
            return (-1j) ** l * q

        def _so3_cg(l1, l2, l3):
            C = np.einsum('ij,kl,mn,ikn->jlm', _qmat(l1), _qmat(l2), np.conj(_qmat(l3)).T, _su2_cg(l1, l2, l3))
            assert np.abs(C.imag).max() < 1e-06
            C = C.real
            return C / np.linalg.norm(C)
        CG = {c: jnp.asarray(_so3_cg(*c), dtype=jnp.float32) for c in COMBOS}
        N, E = (12500, 200000)
        ks = jax.random.split(jax.random.key(seed), 6)
        return {'node_irreps': jax.random.normal(ks[0], (N, 4 * M), jnp.float32), 'edge_index': jax.random.randint(ks[1], (2, E), 0, N, dtype=jnp.int32), 'sh0': jax.random.normal(ks[2], (E, 1), jnp.float32), 'sh1': jax.random.normal(ks[3], (E, 3), jnp.float32), 'sh2': jax.random.normal(ks[4], (E, 5), jnp.float32), 'W': jax.random.normal(ks[5], (len(COMBOS), M, M), jnp.float32)}
    _L1_gnn_all = _L1_gnn_setup()
    _L1_gnn_in = {k: v for k, v in _L1_gnn_all.items() if k in ('W',)}
    del _L1_gnn_all

    def _L2_gnn_setup():
        import jax, jax.numpy as jnp
        import numpy as np
        N_NODES = 12500
        N_EDGES = 400000
        D_IN = 32
        N_HEADS = 4
        D_HEAD = 8
        key = jax.random.key(seed)
        k1, k2, k3, k4, k5, k6, k7 = jax.random.split(key, 7)
        scale = 1.0 / np.sqrt(D_IN)
        x = jax.random.normal(k1, (N_NODES, D_IN), dtype=jnp.float32)
        Wq = jax.random.normal(k2, (D_IN, N_HEADS * D_HEAD), dtype=jnp.float32) * scale
        Wk = jax.random.normal(k3, (D_IN, N_HEADS * D_HEAD), dtype=jnp.float32) * scale
        Wv = jax.random.normal(k4, (D_IN, N_HEADS * D_HEAD), dtype=jnp.float32) * scale
        Wo = jax.random.normal(k5, (N_HEADS * D_HEAD, D_IN), dtype=jnp.float32) * scale
        src = jax.random.randint(k6, (N_EDGES,), 0, N_NODES)
        dst = jax.random.randint(k7, (N_EDGES,), 0, N_NODES)
        edge_index = jnp.stack([src, dst], axis=0).astype(jnp.int64)
        return {'x': x, 'Wq': Wq, 'Wk': Wk, 'Wv': Wv, 'Wo': Wo, 'edge_index': edge_index}
    _L2_gnn_all = _L2_gnn_setup()
    _L2_gnn_in = {k: v for k, v in _L2_gnn_all.items() if k in ('Wq', 'Wk', 'Wv', 'Wo')}
    del _L2_gnn_all

    def _L3_gnn_setup():
        import jax, jax.numpy as jnp
        import numpy as np
        MUL = 8
        N_NODES = 12500
        N_EDGES = 100000
        EDGE_DIM = 32
        MLP_DIM = 64
        W_NUMEL = 4 * MUL * MUL
        ALPHA = 0.25
        C110 = 1.0 / np.sqrt(3.0)
        SI_SCALE = 1.0 / np.sqrt(MUL)
        key = jax.random.key(seed)
        ks = jax.random.split(key, 10)
        node_attr = jax.random.normal(ks[0], (N_NODES, 4 * MUL), dtype=jnp.float32)
        edge_index = jax.random.randint(ks[1], (2, N_EDGES), 0, N_NODES, dtype=jnp.int64)
        edge_sh = jax.random.normal(ks[2], (N_EDGES, 4), dtype=jnp.float32)
        edge_feat = jax.random.normal(ks[3], (N_EDGES, EDGE_DIM), dtype=jnp.float32)
        W1 = jax.random.normal(ks[4], (EDGE_DIM, MLP_DIM), dtype=jnp.float32) / np.sqrt(EDGE_DIM)
        b1 = jnp.zeros((MLP_DIM,), dtype=jnp.float32)
        W2 = jax.random.normal(ks[5], (MLP_DIM, W_NUMEL), dtype=jnp.float32) / np.sqrt(MLP_DIM)
        b2 = jnp.zeros((W_NUMEL,), dtype=jnp.float32)
        si_w0 = jax.random.normal(ks[6], (MUL, MUL), dtype=jnp.float32)
        si_w1 = jax.random.normal(ks[7], (MUL, MUL), dtype=jnp.float32)
        return {'node_attr': node_attr, 'edge_index': edge_index, 'edge_sh': edge_sh, 'edge_feat': edge_feat, 'W1': W1, 'b1': b1, 'W2': W2, 'b2': b2, 'si_w0': si_w0, 'si_w1': si_w1}
    _L3_gnn_all = _L3_gnn_setup()
    _L3_gnn_in = {k: v for k, v in _L3_gnn_all.items() if k in ('W1', 'b1', 'W2', 'b2', 'si_w0', 'si_w1')}
    del _L3_gnn_all
    return {'x': x, 'src': src, 'dst': dst, 'edge_attr_3': edge_attr_3, 'edge_attr_32': edge_attr_32, 'edge_attr_4': edge_attr_4, 'edge_attr_5': edge_attr_5, 'edge_weight1': edge_weight1, 'L1_gnn_W': _L1_gnn_in['W'], 'L2_gnn_Wq': _L2_gnn_in['Wq'], 'L2_gnn_Wk': _L2_gnn_in['Wk'], 'L2_gnn_Wv': _L2_gnn_in['Wv'], 'L2_gnn_Wo': _L2_gnn_in['Wo'], 'L3_gnn_W1': _L3_gnn_in['W1'], 'L3_gnn_b1': _L3_gnn_in['b1'], 'L3_gnn_W2': _L3_gnn_in['W2'], 'L3_gnn_b2': _L3_gnn_in['b2'], 'L3_gnn_si_w0': _L3_gnn_in['si_w0'], 'L3_gnn_si_w1': _L3_gnn_in['si_w1']}

def reference(x, src, dst, edge_attr_3, edge_attr_32, edge_attr_4, edge_attr_5, edge_weight1, L1_gnn_W, L2_gnn_Wq, L2_gnn_Wk, L2_gnn_Wv, L2_gnn_Wo, L3_gnn_W1, L3_gnn_b1, L3_gnn_W2, L3_gnn_b2, L3_gnn_si_w0, L3_gnn_si_w1):
    import jax
    import jax.numpy as jnp

    def _L0_gnn_ref(x, edge_index, num_layers):
        import jax, jax.numpy as jnp
        import numpy as np
        N_NODES = 12500
        N_EDGES = 200000
        LATENT_DIM = 32
        NUM_LAYERS = 3
        N = x.shape[0]
        src = edge_index[0]
        dst = edge_index[1]
        cnt = jax.ops.segment_sum(jnp.ones((edge_index.shape[1],), x.dtype), dst, num_segments=N)
        denom = jnp.maximum(cnt, 1.0)[:, None]
        scale = 1.0 / (num_layers + 1)
        final = x * scale
        for _ in range(num_layers):
            summed = jax.ops.segment_sum(x[src], dst, num_segments=N)
            x = summed / denom
            final = final + x * scale
        return final

    def _L1_gnn_ref(node_irreps, edge_index, sh0, sh1, sh2, W):
        import jax, jax.numpy as jnp
        import numpy as np
        import math
        M = 8
        COMBOS = [(0, 0, 0), (0, 1, 1), (1, 0, 1), (1, 1, 0), (1, 1, 1), (2, 1, 1)]

        def _cg_coeff(j1, m1, j2, m2, j3, m3):
            if m3 != m1 + m2:
                return 0.0
            f = math.factorial
            vmin = max(0, j2 - j3 - m1, j1 + m2 - j3)
            vmax = min(j1 + j2 - j3, j1 - m1, j2 + m2)
            pref = (2 * j3 + 1) * f(j3 + j1 - j2) * f(j3 - j1 + j2) * f(j1 + j2 - j3) / f(j1 + j2 + j3 + 1)
            pref *= f(j3 + m3) * f(j3 - m3) * f(j1 - m1) * f(j1 + m1) * f(j2 - m2) * f(j2 + m2)
            s = 0.0
            for v in range(vmin, vmax + 1):
                s += (-1) ** v / (f(v) * f(j1 + j2 - j3 - v) * f(j1 - m1 - v) * f(j2 + m2 - v) * f(j3 - j2 + m1 + v) * f(j3 - j1 - m2 + v))
            return math.sqrt(pref) * s

        def _su2_cg(l1, l2, l3):
            C = np.zeros((2 * l1 + 1, 2 * l2 + 1, 2 * l3 + 1), dtype=np.complex128)
            for m1 in range(-l1, l1 + 1):
                for m2 in range(-l2, l2 + 1):
                    m3 = m1 + m2
                    if -l3 <= m3 <= l3:
                        C[m1 + l1, m2 + l2, m3 + l3] = _cg_coeff(l1, m1, l2, m2, l3, m3)
            return C

        def _qmat(l):
            q = np.zeros((2 * l + 1, 2 * l + 1), dtype=np.complex128)
            for m in range(-l, 0):
                q[l + m, l + abs(m)] = 1 / np.sqrt(2)
                q[l + m, l - abs(m)] = -1j / np.sqrt(2)
            q[l, l] = 1.0
            for m in range(1, l + 1):
                q[l + m, l + abs(m)] = (-1) ** m / np.sqrt(2)
                q[l + m, l - abs(m)] = 1j * (-1) ** m / np.sqrt(2)
            return (-1j) ** l * q

        def _so3_cg(l1, l2, l3):
            C = np.einsum('ij,kl,mn,ikn->jlm', _qmat(l1), _qmat(l2), np.conj(_qmat(l3)).T, _su2_cg(l1, l2, l3))
            assert np.abs(C.imag).max() < 1e-06
            C = C.real
            return C / np.linalg.norm(C)
        CG = {c: jnp.asarray(_so3_cg(*c), dtype=jnp.float32) for c in COMBOS}
        N, E = (node_irreps.shape[0], edge_index.shape[1])
        src = node_irreps[edge_index[0]]
        feats = {0: src[:, :M][:, :, None], 1: src[:, M:].reshape(E, M, 3)}
        sh = {0: sh0, 1: sh1, 2: sh2}
        msg = {0: jnp.zeros((E, M, 1), node_irreps.dtype), 1: jnp.zeros((E, M, 3), node_irreps.dtype)}
        for idx, (le, ln, lo) in enumerate(COMBOS):
            base = jnp.einsum('ijk,ei,emj->emk', CG[le, ln, lo], sh[le], feats[ln])
            msg[lo] = msg[lo] + jnp.einsum('io,eik->eok', W[idx], base)
        tgt = edge_index[1]
        agg0 = jax.ops.segment_sum(msg[0].reshape(E, M), tgt, num_segments=N)
        agg1 = jax.ops.segment_sum(msg[1].reshape(E, 3 * M), tgt, num_segments=N)
        return jnp.concatenate([agg0, agg1], axis=1)

    def _L2_gnn_ref(x, Wq, Wk, Wv, Wo, edge_index):
        import jax, jax.numpy as jnp
        import numpy as np
        N_NODES = 12500
        N_EDGES = 400000
        D_IN = 32
        N_HEADS = 4
        D_HEAD = 8
        N = x.shape[0]
        src, dst = (edge_index[0], edge_index[1])
        q = (x @ Wq).reshape(N, N_HEADS, D_HEAD)
        k = (x @ Wk).reshape(N, N_HEADS, D_HEAD)
        v = (x @ Wv).reshape(N, N_HEADS, D_HEAD)
        inv_sqrt_d = jnp.asarray(1.0 / np.sqrt(D_HEAD), dtype=x.dtype)
        scores = jnp.einsum('ehd,ehd->eh', q[dst], k[src]) * inv_sqrt_d
        m = jax.ops.segment_max(scores, dst, num_segments=N)
        m = jnp.where(jnp.isfinite(m), m, jnp.zeros_like(m))
        e = jnp.exp(scores - m[dst])
        denom = jax.ops.segment_sum(e, dst, num_segments=N)
        msg = jax.ops.segment_sum(e[:, :, None] * v[src], dst, num_segments=N)
        attn_out = msg / jnp.maximum(denom, 1e-16)[:, :, None]
        out = attn_out.reshape(N, N_HEADS * D_HEAD) @ Wo
        return x + out

    def _L3_gnn_ref(node_attr, edge_index, edge_sh, edge_feat, W1, b1, W2, b2, si_w0, si_w1):
        import jax, jax.numpy as jnp
        import numpy as np
        MUL = 8
        N_NODES = 12500
        N_EDGES = 100000
        EDGE_DIM = 32
        MLP_DIM = 64
        W_NUMEL = 4 * MUL * MUL
        ALPHA = 0.25
        C110 = 1.0 / np.sqrt(3.0)
        SI_SCALE = 1.0 / np.sqrt(MUL)
        n = node_attr.shape[0]
        e = edge_sh.shape[0]
        h = jax.nn.relu(edge_feat @ W1 + b1)
        w = (h @ W2 + b2).reshape(e, 4, MUL, MUL)
        w_000, w_011, w_101, w_110 = (w[:, 0], w[:, 1], w[:, 2], w[:, 3])
        s = node_attr[:, :MUL]
        v = node_attr[:, MUL:].reshape(n, MUL, 3)
        src, dst = (edge_index[0], edge_index[1])
        s_e = s[src]
        v_e = v[src]
        sh0 = edge_sh[:, 0]
        sh1 = edge_sh[:, 1:4]
        m0 = ALPHA * (jnp.einsum('ei,eio->eo', s_e * sh0[:, None], w_000) + C110 * jnp.einsum('eim,em,eio->eo', v_e, sh1, w_110))
        m1 = ALPHA * (jnp.einsum('ei,em,eio->eom', s_e, sh1, w_011) + jnp.einsum('eim,eio->eom', v_e * sh0[:, None, None], w_101))
        out0 = jax.ops.segment_sum(m0, dst, num_segments=n)
        out1 = jax.ops.segment_sum(m1.reshape(e, MUL * 3), dst, num_segments=n).reshape(n, MUL, 3)
        out0 = out0 + SI_SCALE * (s @ si_w0)
        out1 = out1 + SI_SCALE * jnp.einsum('nim,io->nom', v, si_w1)
        return jnp.concatenate([out0, out1.reshape(n, MUL * 3)], axis=-1)
    edge_index = jnp.stack([src, dst])
    h = jnp.maximum(_layernorm(x, axis=-1), 0.0)
    x = x + _L0_gnn_ref(h, edge_index, 3)
    h = jnp.maximum(_layernorm(x, axis=-1), 0.0)
    x = x + _L1_gnn_ref(h, edge_index, edge_weight1, edge_attr_3, edge_attr_5, L1_gnn_W)
    h = jnp.maximum(_layernorm(x, axis=-1), 0.0)
    x = x + _L2_gnn_ref(h, L2_gnn_Wq, L2_gnn_Wk, L2_gnn_Wv, L2_gnn_Wo, edge_index)
    h = jnp.maximum(_layernorm(x, axis=-1), 0.0)
    x = x + _L3_gnn_ref(h, edge_index, edge_attr_4, edge_attr_32, L3_gnn_W1, L3_gnn_b1, L3_gnn_W2, L3_gnn_b2, L3_gnn_si_w0, L3_gnn_si_w1)
    return x

_drawn_inputs = setup_inputs


def setup_inputs(seed=0):
    import zlib

    import numpy as np

    out = dict(_drawn_inputs(seed))
    spreads = {'L3_gnn_b1': (0.0, 0.409), 'L3_gnn_b2': (0.0, 0.305)}
    factors = {'L2_gnn_Wq': 7.506, 'L2_gnn_Wk': 7.909}
    for name, (base, spread) in spreads.items():
        noise = np.random.default_rng([zlib.crc32(name.encode()), seed]).standard_normal(out[name].shape)
        drawn = base * np.exp(spread * noise) if base else spread * noise
        out[name] = jnp.asarray(drawn.astype(out[name].dtype))
    for name, factor in factors.items():
        out[name] = (out[name] * factor).astype(out[name].dtype)
    return out
```

```python
from contextlib import ExitStack

import numpy as np

import concourse.bass as bass
from concourse import mybir

F32 = mybir.dt.float32
I32 = mybir.dt.int32
ALU = mybir.AluOpType
ACT = mybir.ActivationFunctionType
AX = mybir.AxisListType.X
RMAX = bass.bass_isa.ReduceOp.max

P = 128
N, E, D = 12500, 200000, 32
NB = -(-N // P)
NP = NB * P
W = 128
NACC = NP + W
T = 4
ST = T * P
U = 4
NI = -(-E // (ST * U))
S = NI * U
EP = S * ST
NOWHERE = 30000.0
SHK = 9
HEADS, DH = 4, 8
BIG = 1.0e30
FLOOR = -1.0e29
MLP = 64
ALPHA = 0.25
C110 = 1.0 / np.sqrt(3.0)
EPS = 1e-5
BPC = 14
NC = NB // BPC



class Count:

    def __init__(self, sem):
        self.sem, self.n = sem, 0

    def inc(self, ins):
        ins.then_inc(self.sem, 1)
        self.n += 1


def back(here, before, u, skew):
    turn, slot = (here, u - skew) if u >= skew else (before, u - skew + U)
    return None if turn is None else (turn[0], turn[1], slot)


def sweeps(eng, n_sweeps, turn):
    with eng.Fori(0, n_sweeps) as w:
        turn((w * NI, 0), None)
        with eng.Fori(1, NI) as it:
            turn((w * NI + it, it), (w * NI + it - 1, it - 1))
        turn(None, (w * NI + NI - 1, NI - 1))


def number(itg, u):
    return itg * U + u


def build(nc, t):
    with ExitStack() as ctx:
        def sb(name, shape, dt=F32):
            return ctx.enter_context(nc.sbuf_tensor(name, shape, dt))

        def sem(name):
            return ctx.enter_context(nc.semaphore(name))

        def table(name, rows, cols):
            return nc.dram_tensor(name, (rows, cols), F32, kind="Internal").ap()

        psum = ctx.enter_context(nc.psum_tensor("psum", [P, 8, 512], F32))
        acc = sb("acc", [P, NACC])
        peak = sb("peak", [P, NACC])
        X = sb("X", [P, NB, D])
        H = sb("H", [P, NB, D])
        Q = sb("Q", [P, NB, D])
        PROD0 = NB * 2 * D
        FEAT0 = PROD0 + 2 * T * SHK * D
        HIDDEN0 = FEAT0 + U * ST
        SRC0 = HIDDEN0 + 2 * ST
        C = peak[:, 0:NB * D].rearrange("p (b f) -> p b f", b=NB)
        kv_rows = peak[:, 0:NB * 2 * D].rearrange("p (b f) -> p b f", b=NB)
        stat = sb("stat", [P, 4, NB])
        iota = sb("iota", [P, W])
        ident = sb("ident", [P, P])
        dst = sb("dst", [P, S, T])
        rel = sb("rel", [P, S, T])
        base = sb("base", [P, S])
        span = sb("span", [P, S])
        start = sb("start", [P, S])
        off = sb("off", [P, S], I32)
        reach = sb("reach", [P, 2])
        n_sweeps_i = sb("n_sweeps_i", [P, 1], I32)
        onehot = sb("onehot", [P, U, T, W])
        idx = sb("idx", [P, U, T], I32)
        rows = sb("rows", [P, U, T, 64])
        sh = sb("sh", [P, U, T, SHK])
        msg = sb("msg", [P, U, T, 64])
        prod = peak[:, PROD0:FEAT0].rearrange("p (a t k) -> p a t k", a=2, t=T)
        cg = sb("cg", [96, 3, 6, D])
        sel8 = sb("sel8", [8, 96])
        w_l1 = sb("w_l1", [8, 6, 8])
        w_exp = sb("w_exp", [96, 6, D])
        w_fold = sb("w_fold", [96, 3, D])
        w_qkv = sb("w_qkv", [D, 3, D])
        w_o = sb("w_o", [D, D])
        ht = sb("ht", [D, 2, 4 * P])
        pen = sb("pen", [P, U, ST])
        onehot_t = sb("onehot_t", [P, U, ST])
        fold_in = pen[0:96, 0:2, 0:3 * W]
        qwin = sb("qwin", [P, U, D])
        qk = sb("qk", [P, T, D])
        score = sb("score", [P, U, T, HEADS])
        prob = sb("prob", [P, U, T, HEADS])
        masked = sb("masked", [P, ST])
        mloc = sb("mloc", [P, 2, HEADS])
        mrep = sb("mrep", [P, 2, 2, HEADS, DH])
        mnew = sb("mnew", [64, W])
        mdiff = sb("mdiff", [64, 2, W])
        mexp = sb("mexp", [64, 2, W])
        merge = sb("merge", [64, 2, W])
        w1 = sb("w1", [D, MLP])
        b1 = sb("b1", [MLP, 1])
        w2 = sb("w2", [MLP + 1, 256])
        si = sb("si", [8, 2, 8])
        si_mask = sb("si_mask", [D, 2, D])
        si_exp = sb("si_exp", [D, 2, D])
        si_w = sb("si_w", [D, D])
        alpha_i = sb("alpha_i", [D, D])
        feat = peak[0:D, FEAT0:HIDDEN0].rearrange("p (u e) -> p u e", u=U)
        hidden = peak[0:MLP + 1, HIDDEN0:HIDDEN0 + 2 * ST].rearrange("p (u e) -> p u e", u=2)
        src_a = peak[:, SRC0:SRC0 + U * T * D].rearrange("p (u t f) -> p u t f", u=U, t=T)
        src_c = onehot_t[:, 0, 0:U * T * DH].rearrange("p (u t i) -> p u t i", u=U, t=T)
        src_t = onehot_t[:, 1, 0:T * DH * 3].rearrange("p (t k) -> p t k", t=T)
        red = onehot_t[:, 2, 0:T * 6 * DH].rearrange("p (q o) -> p q o", o=DH)
        vec = onehot_t[:, 3, 0:T * DH * 3].rearrange("p (t o m) -> p t o m", t=T, m=3)

        tab = [table(f"tab{k}", NP, D) for k in range(3)]
        tab_tp = table("tab_tp", NP, D)
        tab_kv = table("tab_kv", NP, 2 * D)
        tab_q = table("tab_q", NACC, D)
        tab_cv = table("tab_cv", NP, D)

        loaded = sem("loaded")
        loaded_dst = sem("loaded_dst")
        iota_ready = sem("iota_ready")
        extremes = sem("extremes")
        extremes_all = sem("extremes_all")
        spread_w = sem("spread_w")
        stored = sem("stored")
        node = Count(sem("node"))
        var_ready = sem("var_ready")
        dev_ready = sem("dev_ready")
        marks = {}

        def sems(name, *more):
            p = {k: sem(f"{name}_{k}") for k in
                 ("window_step", "table_ready", "onehot_ready", "scattered", "done", "post_ready") + more
                 if not k.endswith("_loaded")}
            for k in ("idx_loaded", "gathered") + tuple(m for m in more if m.endswith("_loaded")):
                p[k] = [sem(f"{name}_{k}{u}") for u in range(U)]
            return p

        prop = [sems(f"prop{k}", "agg_free") for k in range(3)]
        tp = sems("tp", "agg_free", "sh_loaded", "prod_ready", "fold_copied", "folded")
        at = sems("at", "qwin_loaded", "turned", "turned_copied", "query_ready", "score_step",
                  "score_ready", "spread_ready", "peak_step", "peak_ready", "peak_back", "diff_ready",
                  "prob_ready", "msg_ready", "merge_step", "merge_in", "merge_exp", "merged",
                  "ht_ready", "ht_copied", "proj_ready", "proj_copied", "q_stored")
        cv = sems("cv", "agg_free", "sh_loaded", "feat_loaded", "hidden_ready", "hidden_relu",
                  "weights_ready", "source_step", "prod_step", "msg_ready", "ht_ready", "ht_copied")

        def dram_nodes(dram):
            return dram[0:NP, :].rearrange("(p b) f -> p (b f)", p=P)

        def flat(tile):
            return tile[:, :, :].rearrange("p b f -> p (b f)")

        def blocks_of(c):
            return min(4, NB - 4 * c)

        NQ = -(-NB // 4)
        WSTEPS = 3

        loads = [
            (flat(X), dram_nodes(t["x"])),
            (ident[:, :], t["c_ident"]), (cg[:, :, :, :], t["c_cg"]), (sel8[:, :], t["c_sel"]),
            (si_mask[:, :, :], t["c_si"]),
            (w_l1[:, :, :], t["L1_gnn_W"].rearrange("k i o -> i k o")),
            (w_qkv[:, 0, :], t["L2_gnn_Wq"]), (w_qkv[:, 1, :], t["L2_gnn_Wk"]),
            (w_qkv[:, 2, :], t["L2_gnn_Wv"]), (w_o[:, :], t["L2_gnn_Wo"]),
            (w1[:, :], t["L3_gnn_W1"]), (b1[:, :], t["L3_gnn_b1"].rearrange("(m a) -> m a", a=1)),
            (w2[0:MLP, :], t["L3_gnn_W2"]),
            (w2[MLP:MLP + 1, :], t["L3_gnn_b2"].rearrange("(a m) -> a m", a=1)),
            (si[:, 0, :], t["L3_gnn_si_w0"]), (si[:, 1, :], t["L3_gnn_si_w1"]),
        ]

        block = ctx.enter_context(nc.Block())

        @block.vector
        def _(dve):
            V = nc.vector

            def step(ins):
                node.inc(ins)

            def settle():
                dve.wait_ge(node.sem, node.n)

            def do(ins):
                step(ins)
                settle()

            dve.wait_ge(loaded_dst, 16)
            do(V.tensor_copy(dst[:, :, :], rel[:, :, :].bitcast(I32)))
            do(V.tensor_reduce(base[:, :], dst[:, :, :], AX, ALU.min))
            do(V.tensor_scalar(rel[:, :, :], dst[:, :, :], float(N - 1), None, ALU.min))
            do(V.tensor_reduce(span[:, :], rel[:, :, :], AX, ALU.max))
            V.tensor_scalar(base[:, :], base[:, :], -1.0, None, ALU.mult).then_inc(extremes, 1)
            dve.wait_ge(extremes_all, 2)
            do(V.tensor_scalar(base[:, :], base[:, :], -1.0, None, ALU.mult))
            do(V.tensor_tensor(span[:, :], span[:, :], base[:, :], ALU.subtract))
            do(V.tensor_reduce(reach[:, 0:1], span[:, :], AX, ALU.max))
            dve.wait_ge(iota_ready, 1)
            do(V.tensor_scalar(masked[:, 0:NB], iota[:, 0:NB], float(W), reach[:, 0:1], ALU.mult, ALU.is_le))
            do(V.tensor_reduce(reach[:, 1:2], masked[:, 0:NB], AX, ALU.add))
            do(V.tensor_copy(n_sweeps_i[:, :], reach[:, 1:2]))
            marks["n_sweeps"] = node.n
            n_sweeps = dve.value_load(n_sweeps_i[0:1, 0:1], min_val=1, max_val=NB)

            dve.wait_ge(loaded, 16 * len(loads))
            dve.wait_ge(spread_w, 1)
            for mix, (w_rows, r, k, bank) in enumerate(((w_exp, 96, 6, 0), (si_exp, D, 2, 1))):
                got = psum[0:r, bank, 0:8 * k].rearrange("r (k o) -> r k o", k=k)
                step(V.tensor_copy(w_rows[:, :, 0:8], got))
                for m in range(3):
                    step(V.tensor_copy(w_rows[:, :, 8 + m:D:3], got))
            settle()
            for c in range(3):
                step(V.tensor_tensor(cg[:, c, :, :], cg[:, c, :, :], w_exp[:, :, :], ALU.mult))
            step(V.tensor_tensor(si_mask[:, :, :], si_mask[:, :, :], si_exp[:, :, :], ALU.mult))
            settle()
            for c in range(3):
                step(V.tensor_reduce(w_fold[:, c, :], cg[:, c, :, :].rearrange("r i o -> r o i"), AX, ALU.add))
            step(V.tensor_reduce(si_w[:, :], si_mask[:, :, :].rearrange("r i o -> r o i"), AX, ALU.add))
            step(V.tensor_scalar(alpha_i[:, :], ident[0:D, 0:D], ALPHA, None, ALU.mult))
            step(V.tensor_scalar(w2[:, 192:256], w2[:, 192:256], C110, None, ALU.mult))
            step(V.memset(rows[:, :, :, D:D + 1], 1.0))

            def bnf(x):
                return x.unsqueeze(2).to_broadcast([P, NB, D])

            def layernorm(k):
                do(V.tensor_reduce(stat[:, 0, :], X[:, :, :], AX, ALU.add))
                do(V.tensor_scalar(stat[:, 0, :], stat[:, 0, :], 1.0 / D, None, ALU.mult))
                do(V.tensor_tensor(C, X[:, :, :], bnf(stat[:, 0, :]), ALU.subtract))
                do(V.tensor_tensor(Q[:, :, :], C, C, ALU.mult))
                do(V.tensor_reduce(stat[:, 1, :], Q[:, :, :], AX, ALU.add))
                V.tensor_scalar(stat[:, 1, :], stat[:, 1, :], 1.0 / D, EPS, ALU.mult,
                                ALU.add).then_inc(var_ready, 1)
                dve.wait_ge(dev_ready, k + 1)
                do(V.reciprocal(stat[:, 0, :], stat[:, 2, :]))
                do(V.tensor_tensor(C, C, bnf(stat[:, 0, :]), ALU.mult))
                do(V.tensor_scalar(H[:, :, :], C, 0.0, None, ALU.max))

            def open_windows(p, w):
                V.tensor_scalar(start[:, :], start[:, :], float(W), None, ALU.add).then_inc(p["window_step"], 1)
                dve.wait_ge(p["window_step"], w * WSTEPS + 1)
                V.tensor_tensor(rel[:, :, :], dst[:, :, :], start[:, :].unsqueeze(2).to_broadcast([P, S, T]),
                                ALU.subtract).then_inc(p["window_step"], 1)
                V.tensor_scalar(off[:, :], start[:, :], float(NP), None, ALU.min).then_inc(p["window_step"], 1)
                dve.wait_ge(p["window_step"], (w + 1) * WSTEPS)

            def before_pass(n):
                step(V.tensor_scalar(start[:, :], base[:, :], -float(W), None, ALU.add))
                do(V.memset(acc[0:n, :], 0.0))

            def windowed(p, turn):
                with dve.Fori(0, n_sweeps) as w:
                    open_windows(p, w)
                    turn((w * NI, 0), None)
                    with dve.Fori(1, NI) as it:
                        turn((w * NI + it, it), (w * NI + it - 1, it - 1))
                    turn(None, (w * NI + NI - 1, NI - 1))
                V.drain().then_inc(p["done"], 1)

            def make_onehot(p, itg, it, u):
                g = number(itg, u)
                dve.wait_ge(p["scattered"], g + 1)
                for j in range(T):
                    ins = V.tensor_scalar(onehot[:, u, j, :], iota[:, :],
                                          rel[:, bass.ds(it * U + u, 1), j], None, ALU.is_equal)
                ins.then_inc(p["onehot_ready"], 1)

            def window_column(it, u):
                return dve.value_load(off[0:1, bass.ds(it * U + u, 1)], min_val=0, max_val=NP)

            def add_window(p, k, source, credit, bank, itg, it, u):
                g = number(itg, u)
                window = acc[0:k, bass.ds(window_column(it, u), W)]
                dve.wait_ge(p[source], g + 1 + credit)
                dve.wait_ge(p["agg_free"], g + 2)
                V.tensor_tensor(window, window, psum[0:k, bank + u % 2, 0:W],
                                ALU.add).then_inc(p["agg_free"], 1)

            layernorm(0)
            step(V.tensor_copy(Q[:, :, :], H[:, :, :]))
            for k in range(3):
                p = prop[k]
                settle()
                marks[f"prop{k}"] = node.n
                before_pass(D + 1)
                dve.sem_inc(p["agg_free"], 2)

                def turn(here, before):
                    for u in range(U):
                        if a := back(here, before, u, 0):
                            make_onehot(p, *a)
                        if a := back(here, before, u, 1):
                            add_window(p, D + 1, "scattered", U, 0, *a)
                windowed(p, turn)
                dve.wait_ge(p["table_ready"], 16)
                for c in range(NC):
                    dve.wait_ge(p["post_ready"], c + 1)
                    blk = slice(c * BPC, (c + 1) * BPC)
                    got = psum[:, c, 0:BPC * (D + 1)].rearrange("p (b k) -> p b k", b=BPC)
                    if k == 0:
                        do(V.tensor_scalar(stat[:, 3, blk], got[:, :, D], 1.0, None, ALU.max))
                        do(V.reciprocal(stat[:, 3, blk], stat[:, 3, blk]))
                    step(V.tensor_tensor(H[:, blk, :], got[:, :, 0:D],
                                         stat[:, 3, blk].unsqueeze(2).to_broadcast([P, BPC, D]), ALU.mult))
                settle()
                step(V.tensor_tensor(Q[:, :, :], Q[:, :, :], H[:, :, :], ALU.add))
            settle()
            do(V.scalar_tensor_tensor(X[:, :, :], Q[:, :, :], 0.25, X[:, :, :], ALU.mult, ALU.add))

            layernorm(1)
            marks["tp"] = node.n
            before_pass(D)
            dve.sem_inc(tp["agg_free"], 2)
            dve.sem_inc(tp["prod_ready"], U)

            def multiply(itg, it, u):
                g = number(itg, u)
                dve.wait_ge(tp["gathered"][u], (itg + 1) * 16 * T)
                dve.wait_ge(tp["sh_loaded"][u], (itg + 1) * 16)
                dve.wait_ge(tp["scattered"], g - 1 + U)
                V.tensor_tensor(prod[:, u % 2, :, :].rearrange("p t (j f) -> p t j f", j=SHK),
                                rows[:, u, :, 0:D].unsqueeze(2).to_broadcast([P, T, SHK, D]),
                                sh[:, u, :, :].unsqueeze(3).to_broadcast([P, T, SHK, D]),
                                ALU.mult).then_inc(tp["prod_ready"], 1)

            def tp_turn(here, before):
                for u in range(U):
                    if a := back(here, before, u, 0):
                        make_onehot(tp, *a)
                        multiply(*a)
                    if a := back(here, before, u, 2):
                        add_window(tp, D, "folded", 2, 2, *a)
            windowed(tp, tp_turn)
            for c in range(NC):
                dve.wait_ge(tp["post_ready"], c + 1)
                blk = slice(c * BPC, (c + 1) * BPC)
                step(V.tensor_tensor(X[:, blk, :], X[:, blk, :],
                                     psum[:, c, 0:BPC * D].rearrange("p (b k) -> p b k", b=BPC), ALU.add))
            settle()

            dve.wait_ge(tp["table_ready"], 16)
            layernorm(2)
            marks["at_rows"] = node.n
            step(V.memset(rows[:, 0, 0, 0:D], 0.0))
            settle()
            marks["q_zero"] = node.n
            for c in range(NQ):
                n = blocks_of(c)
                dve.wait_ge(at["proj_ready"], c + 1)
                got = psum[:, 2 + c % 2, 0:96 * n].rearrange("p (b k) -> p b k", b=n)
                V.tensor_scalar(Q[:, 4 * c:4 * c + n, :], got[:, :, 0:D], DH ** -0.5, None, ALU.mult)
                V.tensor_copy(kv_rows[:, 4 * c:4 * c + n, :], got[:, :, D:96]).then_inc(at["proj_copied"], 1)
            step(V.tensor_tensor(X[:, :, :], X[:, :, :], H[:, :, :], ALU.add))
            before_pass(64)
            dve.wait_ge(at["table_ready"], 16)
            do(V.memset(peak[0:64, :], FLOOR))
            for k, r in (("score_ready", 1), ("peak_ready", 1), ("diff_ready", 1), ("msg_ready", U),
                         ("merge_step", 1), ("merge_in", 1), ("merged", 1)):
                dve.sem_inc(at[k], r)

            def at_score(itg, it, u):
                g = number(itg, u)
                dve.wait_ge(at["query_ready"], g + 1)
                dve.wait_ge(at["gathered"][u], (itg + 1) * 16 * T)
                V.tensor_tensor(qk[:, :, :], psum[:, 5, 0:T * D].rearrange("p (t f) -> p t f", t=T),
                                rows[:, u, :, 0:D], ALU.mult).then_inc(at["score_step"], 1)
                dve.wait_ge(at["score_step"], g + 1)
                V.tensor_reduce(score[:, u, :, :].rearrange("p t h -> p (t h)"),
                                qk[:, :, :].rearrange("p t (h d) -> p (t h) d", h=HEADS),
                                AX, ALU.add).then_inc(at["score_ready"], 1)

            def at_peak(itg, it, u):
                g = number(itg, u)
                dve.wait_ge(at["spread_ready"], g + 1)
                dve.wait_ge(at["turned_copied"], g + 2)
                dve.nop(nofuse=True)
                for h in range(HEADS):
                    ins = V.tensor_tensor_reduce(psum[:, 1 + h, :], psum[:, 1 + h, :], pen[:, u, :], 1.0, FLOOR,
                                                 ALU.add, ALU.max, mloc[:, u % 2, h:h + 1])
                ins.then_inc(at["peak_step"], 1)
                dve.wait_ge(at["peak_step"], g + 1)
                V.tensor_copy(mrep[:, u % 2, :, :, :].rearrange("p r h d -> p (r h) d")[:, 0:HEADS, :],
                              mloc[:, u % 2, :].unsqueeze(2).to_broadcast([P, HEADS, DH]))
                V.tensor_copy(mrep[:, u % 2, 1, :, :],
                              mloc[:, u % 2, :].unsqueeze(2).to_broadcast([P, HEADS, DH])
                              ).then_inc(at["peak_ready"], 1)

            def at_shift(itg, it, u):
                g = number(itg, u)
                dve.wait_ge(at["peak_back"], g + 1)
                V.tensor_tensor(prob[:, u, :, :].rearrange("p t h -> p (t h)"),
                                score[:, u, :, :].rearrange("p t h -> p (t h)"),
                                psum[:, 6, 0:T * HEADS], ALU.subtract).then_inc(at["diff_ready"], 1)

            def at_message(itg, it, u):
                g = number(itg, u)
                dve.wait_ge(at["prob_ready"], g + 1)
                p_wide = prob[:, u, :, :].rearrange("p t h -> p (t h)").unsqueeze(2).to_broadcast([P, T * HEADS, DH])
                p_wide = prob[:, u, :, :].unsqueeze(3).to_broadcast([P, T, HEADS, DH])
                V.tensor_tensor(msg[:, u, :, 0:D].rearrange("p t (h d) -> p t h d", h=HEADS),
                                rows[:, u, :, D:2 * D].rearrange("p t (h d) -> p t h d", h=HEADS),
                                p_wide, ALU.mult)
                V.tensor_copy(msg[:, u, :, D:2 * D].rearrange("p t (h d) -> p t h d", h=HEADS),
                              p_wide).then_inc(at["msg_ready"], 1)

            def at_merge_peaks(itg, it, u):
                g = number(itg, u)
                col = window_column(it, u)
                running = peak[0:64, bass.ds(col, W)]
                local = psum[0:64, 6, 128:256]
                dve.wait_ge(at["merge_step"], g * 4 + 1)
                V.tensor_tensor(mnew[:, :], running, local, ALU.max).then_inc(at["merge_step"], 1)
                dve.wait_ge(at["merge_step"], g * 4 + 2)
                V.tensor_tensor(mdiff[:, 0, :], running, mnew[:, :], ALU.subtract)
                V.tensor_tensor(mdiff[:, 1, :], local, mnew[:, :], ALU.subtract).then_inc(at["merge_in"], 1)
                return col

            def at_merge_sums(itg, it, u, col):
                g = number(itg, u)
                sums = acc[0:64, bass.ds(col, W)]
                dve.wait_ge(at["merge_exp"], g + 1)
                dve.wait_ge(at["merged"], g + 1)
                V.tensor_tensor(merge[:, 0, :], sums, mexp[:, 0, :], ALU.mult).then_inc(at["merge_step"], 1)
                V.tensor_copy(peak[0:64, bass.ds(col, W)], mnew[:, :]).then_inc(at["merge_step"], 1)
                dve.wait_ge(at["scattered"], g + 1 + U)
                V.tensor_tensor(merge[:, 1, :], psum[0:64, 7, 0:W], mexp[:, 1, :],
                                ALU.mult).then_inc(at["merge_step"], 1)
                dve.wait_ge(at["merge_step"], g * 4 + 5)
                V.tensor_tensor(sums, merge[:, 0, :], merge[:, 1, :], ALU.add).then_inc(at["merged"], 1)

            def at_turn(here, before):
                for u in range(U):
                    third, second, first = (back(here, before, u, k) for k in (3, 2, 1))
                    if second:
                        at_peak(*second)
                    if first:
                        at_score(*first)
                    if third:
                        col = at_merge_peaks(*third)
                    if a := back(here, before, u, 0):
                        make_onehot(at, *a)
                    if second:
                        at_shift(*second)
                    if third:
                        at_merge_sums(*third, col)
                    if second:
                        at_message(*second)
            windowed(at, at_turn)
            dve.wait_ge(at["done"], 1)
            do(V.tensor_scalar(peak[0:D, 0:NP], acc[D:2 * D, 0:NP], 1e-16, None, ALU.max))
            do(V.reciprocal(peak[0:D, 0:NP], peak[0:D, 0:NP]))
            do(V.tensor_tensor(acc[0:D, 0:NP], acc[0:D, 0:NP], peak[0:D, 0:NP], ALU.mult))
            marks["at_normal"] = node.n
            for c in range(NC):
                dve.wait_ge(at["post_ready"], c + 1)
                blk = slice(c * BPC, (c + 1) * BPC)
                step(V.tensor_tensor(X[:, blk, :], X[:, blk, :],
                                     psum[:, c, 0:BPC * D].rearrange("p (b k) -> p b k", b=BPC), ALU.add))
            settle()

            layernorm(3)
            do(V.memset(hidden[MLP:MLP + 1, :, :], 1.0))
            marks["cv"] = node.n
            before_pass(D)
            for k, r in (("agg_free", 2), ("msg_ready", U), ("source_step", 1)):
                dve.sem_inc(cv[k], r)

            def cv_source(itg, it, u):
                g = number(itg, u)
                dve.wait_ge(cv["gathered"][u], (itg + 1) * 16 * T)
                dve.wait_ge(cv["sh_loaded"][u], (itg + 1) * 16)
                dve.wait_ge(cv["source_step"], g * 2 + 1)
                V.tensor_tensor(src_a[:, u, :, :], rows[:, u, :, 0:D],
                                sh[:, u, :, 0:1].to_broadcast([P, T, D]), ALU.mult)
                V.tensor_tensor(src_t[:, :, :].rearrange("p t (i m) -> p t i m", m=3),
                                rows[:, u, :, DH:D].rearrange("p t (i m) -> p t i m", m=3),
                                sh[:, u, :, 1:4].unsqueeze(2).to_broadcast([P, T, DH, 3]),
                                ALU.mult).then_inc(cv["source_step"], 1)
                dve.wait_ge(cv["source_step"], g * 2 + 2)
                V.tensor_reduce(src_c[:, u, :, :], src_t[:, :, :].rearrange("p t (i m) -> p t i m", m=3),
                                AX, ALU.add).then_inc(cv["source_step"], 1)

            def cv_message(itg, it, u):
                g = number(itg, u)
                dve.wait_ge(cv["weights_ready"], g + 3)
                dve.wait_ge(cv["source_step"], g * 2 + 3)
                dve.wait_ge(cv["msg_ready"], g + U)
                w = psum[:, 1 + 2 * (u % 2):3 + 2 * (u % 2), :].rearrange("p a (t k) -> p (a t) k", t=2)
                products = peak[:, PROD0:PROD0 + T * 384].rearrange(
                    "p (t g k) -> p t g k", t=T, g=6)

                def product(k, weights, source):
                    return V.tensor_tensor(
                        products[:, :, k, :].rearrange("p t (i o) -> p t i o", o=DH),
                        w[:, :, weights * 64:weights * 64 + 64].rearrange("p t (i o) -> p t i o", o=DH),
                        source.unsqueeze(3).to_broadcast([P, T, DH, DH]), ALU.mult)

                product(0, 0, src_a[:, u, :, 0:DH])
                product(1, 3, src_c[:, u, :, :])
                product(2, 1, rows[:, u, :, 0:DH])
                for m in range(3):
                    ins = product(3 + m, 2, src_a[:, u, :, DH + m:D:3])
                ins.then_inc(cv["prod_step"], 1)
                dve.wait_ge(cv["prod_step"], g * 3 + 1)
                V.tensor_reduce(red[:, :, :],
                                products.rearrange("p t g k -> p (t g) k").rearrange("p q (i o) -> p q o i", o=DH),
                                AX, ALU.add).then_inc(cv["prod_step"], 1)
                dve.wait_ge(cv["prod_step"], g * 3 + 2)
                r = red[:, :, :].rearrange("p (t g) o -> p t g o", g=6)
                V.tensor_tensor(vec[:, :, :, :], r[:, :, 2, :].unsqueeze(3).to_broadcast([P, T, DH, 3]),
                                sh[:, u, :, 1:4].unsqueeze(2).to_broadcast([P, T, DH, 3]),
                                ALU.mult).then_inc(cv["prod_step"], 1)
                V.tensor_tensor(msg[:, u, :, 0:DH], r[:, :, 0, :], r[:, :, 1, :], ALU.add)
                dve.wait_ge(cv["prod_step"], g * 3 + 3)
                V.tensor_tensor(msg[:, u, :, DH:D].rearrange("p t (o m) -> p t o m", m=3), vec[:, :, :, :],
                                r[:, :, 3:6, :].rearrange("p t m o -> p t o m"),
                                ALU.add).then_inc(cv["msg_ready"], 1)

            def cv_turn(here, before):
                for u in range(U):
                    if a := back(here, before, u, 0):
                        make_onehot(cv, *a)
                        cv_source(*a)
                    if a := back(here, before, u, 1):
                        cv_message(*a)
                    if a := back(here, before, u, 2):
                        add_window(cv, D, "scattered", U, 5, *a)
            windowed(cv, cv_turn)
            for c in range(NQ):
                n = blocks_of(c)
                dve.wait_ge(cv["post_ready"], c + 1)
                step(V.tensor_tensor(X[:, 4 * c:4 * c + n, :], X[:, 4 * c:4 * c + n, :],
                                     psum[:, 2 + c % 2, 0:n * D].rearrange("p (b k) -> p b k", b=n), ALU.add))
                marks[f"out{c}"] = node.n
            settle()
            marks["out"] = node.n

        @block.sync
        def _(sp):
            sp.dma_start(rel[:, :, :].bitcast(I32), t["dst"]).then_inc(loaded_dst, 16)
            for out_ap, in_ap in loads:
                sp.dma_start(out_ap, in_ap).then_inc(loaded, 16)
            sp.wait_ge(node.sem, marks["n_sweeps"])
            n_sweeps = sp.value_load(n_sweeps_i[0:1, 0:1], min_val=1, max_val=NB)

            def load_idx(p, slot_free, itg, it, u):
                sp.wait_ge(p[slot_free], number(itg, u) + 1)
                sp.dma_start(idx[:, u, :], t["src"][bass.ds(it * U + u, 1)].rearrange("a p t -> (a p) t")
                             ).then_inc(p["idx_loaded"][u], 16)

            def every_supertile(load):
                with sp.Fori(0, n_sweeps) as w:
                    with sp.Fori(0, NI) as it:
                        for u in range(U):
                            load(w * NI + it, it, u)

            for k in range(3):
                sp.wait_ge(node.sem, marks[f"prop{k}"])
                sp.dma_start(dram_nodes(tab[k]), flat(H)).then_inc(prop[k]["table_ready"], 16)
                every_supertile(lambda *a: load_idx(prop[k], "scattered", *a))

            sp.wait_ge(node.sem, marks["tp"])
            sp.dma_start(dram_nodes(tab_tp), flat(H)).then_inc(tp["table_ready"], 16)

            def tp_load(itg, it, u):
                load_idx(tp, "prod_ready", itg, it, u)
                sp.dma_start(sh[:, u, :, :], t["sh"][bass.ds(it * U + u, 1)].rearrange("a p t k -> (a p) t k")
                             ).then_inc(tp["sh_loaded"][u], 16)
            every_supertile(tp_load)

            sp.wait_ge(node.sem, marks["q_zero"])
            sp.dma_start(tab_q[NP:NACC, :], rows[:, 0, 0, 0:D]).then_inc(at["q_stored"], 16)
            sp.wait_ge(at["proj_copied"], NQ)
            sp.dma_start(dram_nodes(tab_kv), flat(kv_rows)).then_inc(at["table_ready"], 16)
            sp.dma_start(dram_nodes(tab_q), flat(Q)).then_inc(at["q_stored"], 16)
            sp.wait_ge(at["q_stored"], 32)
            with sp.Fori(0, n_sweeps) as w:
                sp.wait_ge(at["window_step"], (w + 1) * WSTEPS)
                sp.nop(nofuse=True)
                with sp.Fori(0, NI) as it:
                    for u in range(U):
                        load_idx(at, "msg_ready", w * NI + it, it, u)
                        col = sp.value_load(off[0:1, bass.ds(it * U + u, 1)], min_val=0, max_val=NP)
                        sp.dma_start(qwin[:, u, :], tab_q[bass.ds(col, W), :]).then_inc(at["qwin_loaded"][u], 16)

            sp.wait_ge(node.sem, marks["cv"])
            sp.dma_start(dram_nodes(tab_cv), flat(H)).then_inc(cv["table_ready"], 16)

            def cv_load(itg, it, u):
                load_idx(cv, "msg_ready", itg, it, u)
                sp.dma_start(sh[:, u, :, 0:4], t["attr4"][bass.ds(it * U + u, 1)].rearrange("a p t k -> (a p) t k")
                             ).then_inc(cv["sh_loaded"][u], 16)
                sp.dma_start(feat[:, u, :], t["feat"][bass.ds(it * U + u, 1)].rearrange("a f e -> (a f) e")
                             ).then_inc(cv["feat_loaded"][u], 16)
            every_supertile(cv_load)

            sp.wait_ge(node.sem, marks["out"])
            sp.dma_start(dram_nodes(t["out"]), flat(X)).then_inc(stored, 16)
            sp.wait_ge(stored, 16)

        @block.gpsimd
        def _(pool):
            pool.iota(iota[:, :], pattern=[[1, W]], base=0, channel_multiplier=0,
                      allow_small_or_imprecise_dtypes=True).then_inc(iota_ready, 1)
            pool.wait_ge(extremes, 1)
            nc.gpsimd.partition_all_reduce(base[:, :], base[:, :], P, RMAX).then_inc(extremes_all, 1)
            nc.gpsimd.partition_all_reduce(span[:, :], span[:, :], P, RMAX).then_inc(extremes_all, 1)
            pool.wait_ge(node.sem, marks["n_sweeps"])
            n_sweeps = pool.value_load(n_sweeps_i[0:1, 0:1], min_val=1, max_val=NB)
            for p, source, width in ((prop[0], tab[0], D), (prop[1], tab[1], D), (prop[2], tab[2], D),
                                     (tp, tab_tp, D), (at, tab_kv, 2 * D), (cv, tab_cv, D)):
                pool.wait_ge(p["table_ready"], 16)
                with pool.Fori(0, n_sweeps) as w:
                    with pool.Fori(0, NI) as it:
                        for u in range(U):
                            pool.wait_ge(p["idx_loaded"][u], (w * NI + it + 1) * 16)
                            pool.nop(nofuse=True)
                            for j in range(T):
                                pool.indirect_dma_start(
                                    rows[:, u, j, 0:width], None, source[:, :],
                                    bass.IndirectOffsetOnAxis(ap=idx[:, u, j:j + 1], axis=0)
                                ).then_inc(p["gathered"][u], 16)

        @block.scalar
        def _(act):
            A = nc.scalar
            act.wait_ge(node.sem, marks["n_sweeps"])
            n_sweeps = act.value_load(n_sweeps_i[0:1, 0:1], min_val=1, max_val=NB)

            def deviation(k):
                act.wait_ge(var_ready, k + 1)
                A.activation(stat[:, 2, :], stat[:, 1, :], ACT.Sqrt).then_inc(dev_ready, 1)

            deviation(0)
            deviation(1)

            act.sem_inc(tp["fold_copied"], 2)

            def tp_turn(here, before):
                for u in range(U):
                    if a := back(here, before, u, 0):
                        itg, it, slot = a
                        g = number(itg, slot)
                        act.wait_ge(tp["scattered"], g + 1 + U)
                        act.wait_ge(tp["folded"], g + 1)
                        A.activation(fold_in[:, slot % 2, :], psum[0:96, slot % 2, 0:3 * W],
                                     ACT.Copy).then_inc(tp["fold_copied"], 1)
            sweeps(act, n_sweeps, tp_turn)

            deviation(2)

            def copy_turned_rows(p):
                for c in range(NQ):
                    act.wait_ge(p["ht_ready"], c + 1)
                    if c >= 2:
                        act.wait_ge(p["proj_ready" if p is at else "post_ready"], c - 1)
                    A.activation(ht[:, c % 2, 0:blocks_of(c) * P], psum[0:D, c % 2, 0:blocks_of(c) * P],
                                 ACT.Copy).then_inc(p["ht_copied"], 1)

            copy_turned_rows(at)
            act.sem_inc(at["turned_copied"], 1)

            def at_turn(here, before):
                for u in range(U):
                    if a := back(here, before, u, 3):
                        g = number(a[0], a[2])
                        act.wait_ge(at["merge_in"], g + 2)
                        act.wait_ge(at["merged"], g + 1)
                        A.activation(mexp[:, :, :], mdiff[:, :, :], ACT.Exp).then_inc(at["merge_exp"], 1)
                    if a := back(here, before, u, 2):
                        g = number(a[0], a[2])
                        act.wait_ge(at["diff_ready"], g + 2)
                        A.activation(prob[:, a[2], :, :], prob[:, a[2], :, :], ACT.Exp).then_inc(at["prob_ready"], 1)
                    if a := back(here, before, u, 0):
                        g = number(a[0], a[2])
                        act.wait_ge(at["turned"], g + 1)
                        act.wait_ge(at["msg_ready"], g + 1)
                        A.activation(onehot_t[:, a[2], :], psum[:, 0, :], ACT.Copy)
                        A.activation(pen[:, a[2], :], psum[:, 0, :], ACT.Copy, bias=-BIG,
                                     scale=BIG).then_inc(at["turned_copied"], 1)
            sweeps(act, n_sweeps, at_turn)

            deviation(3)

            def cv_turn(here, before):
                for u in range(U):
                    if a := back(here, before, u, 0):
                        g = number(a[0], a[2])
                        act.wait_ge(cv["hidden_ready"], g + 1)
                        act.wait_ge(cv["weights_ready"], g + 1)
                        A.activation(hidden[0:MLP, a[2] % 2, :], psum[0:MLP, 0, :], ACT.Relu,
                                     bias=b1[:, 0:1]).then_inc(cv["hidden_relu"], 1)
            act.sem_inc(cv["hidden_relu"], 1)
            sweeps(act, n_sweeps, cv_turn)
            copy_turned_rows(cv)

        @block.tensor
        def _(pe):
            M = nc.tensor
            pe.wait_ge(loaded, 16 * len(loads))
            M.matmul(psum[0:96, 0, 0:48], sel8[:, :], w_l1[:, :, :].rearrange("i k o -> i (k o)"),
                     start=True, stop=True)
            M.matmul(psum[0:D, 1, 0:16], sel8[:, 0:D], si[:, :, :].rearrange("i k o -> i (k o)"),
                     start=True, stop=True).then_inc(spread_w, 1)
            pe.wait_ge(node.sem, marks["n_sweeps"])
            n_sweeps = pe.value_load(n_sweeps_i[0:1, 0:1], min_val=1, max_val=NB)

            def rows_of_acc(p, k, times):
                for c in range(NC):
                    for j in range(BPC):
                        ins = M.matmul(psum[:, c, j * k:(j + 1) * k], acc[0:k, c * BPC + j:NP:NB],
                                       times, start=True, stop=True)
                    ins.then_inc(p["post_ready"], 1)

            for k in range(3):
                p = prop[k]
                pe.sem_inc(p["scattered"], U)

                def turn(here, before):
                    for u in range(U):
                        if a := back(here, before, u, 0):
                            g = number(a[0], a[2])
                            pe.wait_ge(p["gathered"][u], (a[0] + 1) * 16 * T)
                            pe.wait_ge(p["onehot_ready"], g + 1)
                            pe.wait_ge(p["agg_free"], g + 1)
                            for j in range(T):
                                ins = M.matmul(psum[0:D + 1, u % 2, 0:W], rows[:, u, j, 0:D + 1],
                                               onehot[:, u, j, :], start=(j == 0), stop=(j == T - 1))
                            ins.then_inc(p["scattered"], 1)
                sweeps(pe, n_sweeps, turn)
                pe.wait_ge(p["done"], 1)
                rows_of_acc(p, D + 1, ident[0:D + 1, 0:D + 1])

            pe.sem_inc(tp["scattered"], U)
            pe.sem_inc(tp["folded"], 2)

            def tp_turn(here, before):
                for u in range(U):
                    if a := back(here, before, u, 1):
                        g, s = number(a[0], a[2]), a[2]
                        pe.wait_ge(tp["fold_copied"], g + 3)
                        pe.wait_ge(tp["agg_free"], g + 1)
                        for c in range(3):
                            ins = M.matmul(psum[0:D, 2 + s % 2, 0:W], w_fold[:, c, :],
                                           fold_in[:, s % 2, c * W:(c + 1) * W], start=(c == 0), stop=(c == 2))
                        ins.then_inc(tp["folded"], 1)
                    if a := back(here, before, u, 0):
                        g, s = number(a[0], a[2]), a[2]
                        pe.wait_ge(tp["onehot_ready"], g + 1)
                        pe.wait_ge(tp["prod_ready"], g + 1 + U)
                        pe.wait_ge(tp["fold_copied"], g + 1)
                        for c in range(3):
                            for j in range(T):
                                ins = M.matmul(psum[0:96, s % 2, c * W:(c + 1) * W],
                                               prod[:, s % 2, j, c * 96:(c + 1) * 96],
                                               onehot[:, s, j, :], start=(j == 0), stop=(j == T - 1))
                        ins.then_inc(tp["scattered"], 1)
            sweeps(pe, n_sweeps, tp_turn)
            pe.wait_ge(tp["done"], 1)
            rows_of_acc(tp, D, ident[0:D, 0:D])

            def turn_rows(p, c):
                for j in range(blocks_of(c)):
                    ins = M.transpose(psum[0:D, c % 2, j * P:(j + 1) * P], H[:, 4 * c + j, :], ident[:, :])
                ins.then_inc(p["ht_ready"], 1)

            pe.wait_ge(node.sem, marks["at_rows"])
            for c in range(NQ + 1):
                if c < NQ:
                    if c >= 2:
                        pe.wait_ge(at["ht_copied"], c - 1)
                    turn_rows(at, c)
                if c >= 1:
                    pe.wait_ge(at["ht_copied"], c)
                    if c >= 3:
                        pe.wait_ge(at["proj_copied"], c - 2)
                    for j in range(blocks_of(c - 1)):
                        ins = M.matmul(psum[:, 2 + (c - 1) % 2, j * 96:(j + 1) * 96],
                                       ht[:, (c - 1) % 2, j * P:(j + 1) * P],
                                       w_qkv[:, :, :].rearrange("i k o -> i (k o)"), start=True, stop=True)
                    ins.then_inc(at["proj_ready"], 1)

            pe.sem_inc(at["scattered"], U)

            def at_turn(here, before):
                for u in range(U):
                    first, second, third = (back(here, before, u, k) for k in (1, 2, 3))
                    if first:
                        g, s = number(first[0], first[2]), first[2]
                        pe.wait_ge(at["turned_copied"], g + 2)
                        pe.wait_ge(at["qwin_loaded"][s], (first[0] + 1) * 16)
                        pe.wait_ge(at["score_ready"], g + 1)
                        for j in range(T):
                            ins = M.matmul(psum[:, 5, j * D:(j + 1) * D], onehot_t[:, s, j * P:(j + 1) * P],
                                           qwin[:, s, :], start=True, stop=True)
                        ins.then_inc(at["query_ready"], 1)
                    if third:
                        g, s = number(third[0], third[2]), third[2]
                        pe.wait_ge(at["msg_ready"], g + 1 + U)
                        pe.wait_ge(at["merged"], g + 1)
                        for j in range(T):
                            ins = M.matmul(psum[0:64, 7, 0:W], msg[:, s, j, :], onehot[:, s, j, :],
                                           start=(j == 0), stop=(j == T - 1))
                        ins.then_inc(at["scattered"], 1)
                    if second:
                        g, s = number(second[0], second[2]), second[2]
                        pe.wait_ge(at["peak_ready"], g + 2)
                        pe.wait_ge(at["diff_ready"], g + 1)
                        pe.wait_ge(at["merge_in"], g + 1)
                        for j in range(T):
                            M.matmul(psum[:, 6, j * HEADS:(j + 1) * HEADS], onehot_t[:, s, j * P:(j + 1) * P],
                                     mloc[:, s % 2, :], start=True, stop=True)
                        M.transpose(psum[0:64, 6, 128:256],
                                    mrep[:, s % 2, :, :, :].rearrange("p r h d -> p (r h d)"),
                                    ident[:, :]).then_inc(at["peak_back"], 1)
                    if first:
                        g, s = number(first[0], first[2]), first[2]
                        pe.wait_ge(at["score_ready"], g + 2)
                        pe.wait_ge(at["peak_ready"], g + 1)
                        for h in range(HEADS):
                            for j in range(T):
                                ins = M.transpose(psum[:, 1 + h, j * P:(j + 1) * P],
                                                  score[:, s, j, h:h + 1].to_broadcast([P, P]), ident[:, :])
                        ins.then_inc(at["spread_ready"], 1)
                    if a := back(here, before, u, 0):
                        g, s = number(a[0], a[2]), a[2]
                        pe.wait_ge(at["onehot_ready"], g + 1)
                        pe.wait_ge(at["turned_copied"], g + 1)
                        for j in range(T):
                            ins = M.transpose(psum[:, 0, j * P:(j + 1) * P], onehot[:, s, j, :], ident[:, :])
                        ins.then_inc(at["turned"], 1)
            sweeps(pe, n_sweeps, at_turn)
            pe.wait_ge(node.sem, marks["at_normal"])
            rows_of_acc(at, D, w_o[:, :])

            pe.sem_inc(cv["scattered"], U)
            pe.sem_inc(cv["weights_ready"], 2)

            def cv_turn(here, before):
                for u in range(U):
                    if a := back(here, before, u, 1):
                        g, s = number(a[0], a[2]), a[2]
                        pe.wait_ge(cv["hidden_relu"], g + 2)
                        pe.wait_ge(cv["msg_ready"], g - 1 + U)
                        for j in range(T):
                            ins = M.matmul(psum[:, 1 + 2 * (s % 2) + j // 2, j % 2 * 256:(j % 2 + 1) * 256],
                                           hidden[:, s % 2, j * P:(j + 1) * P], w2[:, :], start=True, stop=True)
                        ins.then_inc(cv["weights_ready"], 1)
                    if a := back(here, before, u, 2):
                        g, s = number(a[0], a[2]), a[2]
                        pe.wait_ge(cv["msg_ready"], g + 1 + U)
                        pe.wait_ge(cv["agg_free"], g + 1)
                        for j in range(T):
                            ins = M.matmul(psum[0:D, 5 + s % 2, 0:W], msg[:, s, j, 0:D], onehot[:, s, j, :],
                                           start=(j == 0), stop=(j == T - 1))
                        ins.then_inc(cv["scattered"], 1)
                    if a := back(here, before, u, 0):
                        g, s = number(a[0], a[2]), a[2]
                        pe.wait_ge(cv["feat_loaded"][s], (a[0] + 1) * 16)
                        pe.wait_ge(cv["hidden_relu"], g + 1)
                        M.matmul(psum[0:MLP, 0, :], w1[:, :], feat[:, s, :], start=True,
                                 stop=True).then_inc(cv["hidden_ready"], 1)
            pe.wait_ge(node.sem, marks["cv"])
            sweeps(pe, n_sweeps, cv_turn)
            pe.wait_ge(cv["done"], 1)
            for c in range(NQ + 1):
                if c < NQ:
                    if c >= 2:
                        pe.wait_ge(cv["ht_copied"], c - 1)
                    turn_rows(cv, c)
                if c >= 1:
                    pe.wait_ge(cv["ht_copied"], c)
                    if c >= 3:
                        pe.wait_ge(node.sem, marks[f"out{c - 3}"])
                    for j in range(blocks_of(c - 1)):
                        here = psum[:, 2 + (c - 1) % 2, j * D:(j + 1) * D]
                        M.matmul(here, ht[:, (c - 1) % 2, j * P:(j + 1) * P], si_w[:, :],
                                 start=True, stop=False)
                        ins = M.matmul(here, acc[0:D, 4 * (c - 1) + j:NP:NB], alpha_i[:, :],
                                       start=False, stop=True)
                    ins.then_inc(cv["post_ready"], 1)


def _coupling():
    import math

    def cg_coeff(j1, m1, j2, m2, j3, m3):
        if m3 != m1 + m2:
            return 0.0
        f = math.factorial
        vmin = max(0, j2 - j3 - m1, j1 + m2 - j3)
        vmax = min(j1 + j2 - j3, j1 - m1, j2 + m2)
        pref = (2 * j3 + 1) * f(j3 + j1 - j2) * f(j3 - j1 + j2) * f(j1 + j2 - j3) / f(j1 + j2 + j3 + 1)
        pref *= f(j3 + m3) * f(j3 - m3) * f(j1 - m1) * f(j1 + m1) * f(j2 - m2) * f(j2 + m2)
        s = 0.0
        for v in range(vmin, vmax + 1):
            s += (-1) ** v / (f(v) * f(j1 + j2 - j3 - v) * f(j1 - m1 - v) * f(j2 + m2 - v)
                              * f(j3 - j2 + m1 + v) * f(j3 - j1 - m2 + v))
        return math.sqrt(pref) * s

    def su2(l1, l2, l3):
        c = np.zeros((2 * l1 + 1, 2 * l2 + 1, 2 * l3 + 1), dtype=np.complex128)
        for m1 in range(-l1, l1 + 1):
            for m2 in range(-l2, l2 + 1):
                if -l3 <= m1 + m2 <= l3:
                    c[m1 + l1, m2 + l2, m1 + m2 + l3] = cg_coeff(l1, m1, l2, m2, l3, m1 + m2)
        return c

    def qmat(n):
        q = np.zeros((2 * n + 1, 2 * n + 1), dtype=np.complex128)
        for m in range(-n, 0):
            q[n + m, n + abs(m)] = 1 / np.sqrt(2)
            q[n + m, n - abs(m)] = -1j / np.sqrt(2)
        q[n, n] = 1.0
        for m in range(1, n + 1):
            q[n + m, n + abs(m)] = (-1) ** m / np.sqrt(2)
            q[n + m, n - abs(m)] = 1j * (-1) ** m / np.sqrt(2)
        return (-1j) ** n * q

    cg = np.zeros((96, 3, 6, D), np.float32)
    first = (0, 1, 4)
    for mix, (le, ln, lo) in enumerate(((0, 0, 0), (0, 1, 1), (1, 0, 1), (1, 1, 0), (1, 1, 1), (2, 1, 1))):
        c = np.einsum("ij,kl,mn,ikn->jlm", qmat(le), qmat(ln), np.conj(qmat(lo)).T, su2(le, ln, lo)).real
        c = c / np.linalg.norm(c)
        for a in range(2 * le + 1):
            j = first[le] + a
            for b in range(2 * ln + 1):
                for i in range(8):
                    f = i if ln == 0 else 8 + 3 * i + b
                    for k in range(2 * lo + 1):
                        outs = slice(0, 8) if lo == 0 else slice(8 + k, D, 3)
                        cg[32 * (j % 3) + f, j // 3, mix, outs] = c[a, b, k]
    si = np.zeros((D, 2, D), np.float32)
    si[0:8, 0, 0:8] = 8 ** -0.5
    for m in range(3):
        si[8 + m::3, 1, 8 + m::3] = 8 ** -0.5
    sel = np.zeros((8, 96), np.float32)
    for r in range(96):
        f = r % D
        sel[f if f < 8 else (f - 8) // 3, r] = 1.0
    return cg, si, sel


_WEIGHTS = ["L1_gnn_W", "L2_gnn_Wq", "L2_gnn_Wk", "L2_gnn_Wv", "L2_gnn_Wo", "L3_gnn_W1", "L3_gnn_b1",
            "L3_gnn_W2", "L3_gnn_b2", "L3_gnn_si_w0", "L3_gnn_si_w1"]


def kernel(**inputs):
    import numpy as _np
    import concourse.bacc as _bacc
    from concourse import mybir as _mybir
    from concourse.bass_utils import run_bass_kernel_spmd as _run

    def edges(name, fill=0):
        a = _np.asarray(inputs[name])
        a = a.reshape(a.shape[0], -1)
        a = _np.concatenate([a, _np.full((EP - E, a.shape[1]), fill, a.dtype)])
        return a.reshape(S, P, T, -1)

    x = _np.asarray(inputs["x"])
    cg, si, sel = _coupling()
    arrays = {
        "x": _np.concatenate([x, _np.zeros((NP - N, D), x.dtype)]),
        "src": edges("src")[..., 0],
        "dst": edges("dst", int(NOWHERE))[..., 0].transpose(1, 0, 2),
        "sh": _np.concatenate([edges("edge_weight1"), edges("edge_attr_3"), edges("edge_attr_5")], axis=-1),
        "attr4": edges("edge_attr_4"),
        "feat": edges("edge_attr_32").transpose(0, 3, 2, 1).reshape(S, D, ST),
        "c_ident": _np.eye(P, dtype=_np.float32),
        "c_cg": cg, "c_si": si, "c_sel": sel,
    }
    for name in _WEIGHTS:
        arrays[name] = _np.asarray(inputs[name])
    nc = _bacc.Bacc("TRN2", target_bir_lowering=False, num_devices=1)
    t, ins = {}, {}
    for name, a in arrays.items():
        ins[f"in_{name}"] = _np.ascontiguousarray(a)
        t[name] = nc.dram_tensor(f"in_{name}", a.shape, _mybir.dt.from_np(a.dtype), kind="ExternalInput").ap()
    t["out"] = nc.dram_tensor("out_0", (NP, D), F32, kind="ExternalOutput").ap()
    build(nc, t)
    r = _run(nc, [ins], core_ids=[0])
    return r.results[0]["out_0"][0:N]
```

```python
from contextlib import ExitStack

import numpy as np

import concourse.bass as bass
from concourse import mybir

F32 = mybir.dt.float32
BF16 = mybir.dt.bfloat16
I32 = mybir.dt.int32
ALU = mybir.AluOpType
ACT = mybir.ActivationFunctionType
AX = mybir.AxisListType.X
RMAX = bass.bass_isa.ReduceOp.max

P = 128
N, E, D = 12500, 200000, 32
NB = -(-N // P)
NP = NB * P
W = 64
NACC = NP + W
T = 3
ST = T * P
U = 4
NI = -(-E // (ST * U))
S = NI * U
EP = S * ST
NOWHERE = 30000.0
SHK = 9
HEADS, DH = 4, 8
BIG = 1.0e30
FLOOR = -1.0e29
MLP = 64
ALPHA = 0.25
C110 = 1.0 / np.sqrt(3.0)
EPS = 1e-5
BPC = 14
NC = NB // BPC



class Count:

    def __init__(self, sem):
        self.sem, self.n = sem, 0

    def inc(self, ins):
        ins.then_inc(self.sem, 1)
        self.n += 1


def back(here, before, u, skew):
    turn, slot = (here, u - skew) if u >= skew else (before, u - skew + U)
    return None if turn is None else (turn[0], turn[1], slot)


def sweeps(eng, n_sweeps, turn):
    with eng.Fori(0, n_sweeps) as w:
        turn((w * NI, 0), None)
        with eng.Fori(1, NI) as it:
            turn((w * NI + it, it), (w * NI + it - 1, it - 1))
        turn(None, (w * NI + NI - 1, NI - 1))


def number(itg, u):
    return itg * U + u


def build(nc, t):
    with ExitStack() as ctx:
        def sb(name, shape, dt=F32):
            return ctx.enter_context(nc.sbuf_tensor(name, shape, dt))

        def sem(name):
            return ctx.enter_context(nc.semaphore(name))

        def table(name, rows, cols):
            return nc.dram_tensor(name, (rows, cols), F32, kind="Internal").ap()

        psum = ctx.enter_context(nc.psum_tensor("psum", [P, 8, 512], F32))
        acc = sb("acc", [P, NACC])
        peak = sb("peak", [P, NACC])
        X = sb("X", [P, NB, D])
        H = sb("H", [P, NB, D])
        Q = sb("Q", [P, NB, D])
        PROD0 = NB * 2 * D
        FEAT0 = PROD0 + 2 * T * SHK * D
        HIDDEN0 = FEAT0 + U * ST
        SRC0 = HIDDEN0 + 2 * ST
        C = peak[:, 0:NB * D].rearrange("p (b f) -> p b f", b=NB)
        psum16 = psum[:, 3, 0:256].bitcast(BF16)
        kv_rows = peak[:, 0:NB * 2 * D].rearrange("p (b f) -> p b f", b=NB)
        stat = sb("stat", [P, 4, NB])
        iota = sb("iota", [P, P])
        ident = sb("ident", [P, P])
        dst = sb("dst", [P, S, T])
        rel = sb("rel", [P, S, T])
        base = sb("base", [P, S])
        span = sb("span", [P, S])
        start = sb("start", [P, S])
        off = sb("off", [P, S], I32)
        reach = sb("reach", [P, 2])
        n_sweeps_i = sb("n_sweeps_i", [P, 1], I32)
        onehot = sb("onehot", [P, U, T, 2 * W])
        dist = sb("dist", [P, T * W])
        one = sb("one", [P, 1])
        idx = sb("idx", [P, U, T], I32)
        rows = sb("rows", [P, U, T, 64])
        sh = sb("sh", [P, U, T, SHK])
        msg = sb("msg", [P, U, T, 64])
        prod = peak[:, PROD0:FEAT0].rearrange("p (a t k) -> p a t k", a=2, t=T)
        w_fold = sb("w_fold", [96, 3, D])
        w_qkv = sb("w_qkv", [D, 3, D])
        w_o = sb("w_o", [D, D])
        ht = sb("ht", [D, 2, 4 * P])
        pen = sb("pen", [2 * W, U, ST])
        onehot_t = sb("onehot_t", [2 * W, U, ST])
        onehot16 = sb("onehot16", [2 * W, 2, ST], BF16)
        CG, EXP = 3 * 6 * D, 6 * D
        lent = onehot_t[:, :, :].rearrange("p u e -> p (u e)")
        cg = lent[0:96, 0:CG].rearrange("r (c i o) -> r c i o", c=3, i=6)
        w_exp = lent[0:96, CG:CG + EXP].rearrange("r (i o) -> r i o", i=6)
        sel8 = lent[0:8, CG + EXP:CG + EXP + 96]
        w_l1 = lent[0:8, CG + EXP + 96:CG + EXP + 144].rearrange("r (k o) -> r k o", k=6)
        si_mask = lent[0:D, CG + EXP + 144:CG + EXP + 208].rearrange("r (i o) -> r i o", i=2)
        si_exp = lent[0:D, CG + EXP + 208:CG + EXP + 272].rearrange("r (i o) -> r i o", i=2)
        fold_in = pen[0:96, 0:2, 0:3 * W]
        qwin = sb("qwin", [2 * W, U, 2 * D], BF16)
        Q16 = peak[:, NB * 2 * D:NB * 2 * D + NB * 3 * D // 2].bitcast(BF16).rearrange("p (b f) -> p b f", b=NB)
        qk = sb("qk", [P, T, D])
        score = sb("score", [P, U, T, HEADS])
        diff = sb("diff", [P, U, T, HEADS])
        masked = sb("masked", [P, 2 * P])
        parts = sb("parts", [P, 2, T, 3 * HEADS], BF16)
        rest = sb("rest", [P, T, HEADS])
        parts_t = sb("parts_t", [3 * HEADS, ST], BF16)
        pick = sb("pick", [3 * HEADS, 2, 2 * W], BF16)
        ident16 = sb("ident16", [P, P], BF16)
        mloc = sb("mloc", [2 * W, 2, 2])
        mrep = sb("mrep", [2 * W, 2, 64])
        both = sb("both", [2 * W, W])
        mdiff = sb("mdiff", [64, W])
        mrelu = sb("mrelu", [64, 2, W])
        mexp = sb("mexp", [64, 2, W])
        merge = sb("merge", [64, 2, W])
        w1 = sb("w1", [D, MLP])
        b1 = sb("b1", [MLP, 1])
        w2 = sb("w2", [MLP + 1, 256])
        si = sb("si", [8, 2, 8])
        si_w = sb("si_w", [D, D])
        alpha_i = sb("alpha_i", [D, D])
        feat = peak[0:D, FEAT0:HIDDEN0].rearrange("p (u e) -> p u e", u=U)
        hidden = peak[0:MLP + 1, HIDDEN0:HIDDEN0 + 2 * ST].rearrange("p (u e) -> p u e", u=2)
        source = peak[:, SRC0:SRC0 + U * T * 48].rearrange("p (u t f) -> p u t f", u=U, t=T)
        src_t = onehot_t[:, 1, 0:T * DH * 3].rearrange("p (t k) -> p t k", t=T)
        red = onehot_t[:, 2, 0:T * 6 * DH].rearrange("p (q o) -> p q o", o=DH)
        vec = onehot_t[:, 3, 0:T * DH * 3].rearrange("p (t o m) -> p t o m", t=T, m=3)

        tab = [table(f"tab{k}", NP, D) for k in range(3)]
        tab_tp = table("tab_tp", NP, D)
        tab_kv = table("tab_kv", NP, 2 * D)
        tab_q = nc.dram_tensor("tab_q", (NACC, 3 * D), BF16, kind="Internal").ap()
        tab_cv = table("tab_cv", NP, D)
        tab_den = table("tab_den", HEADS, NP)
        tab_inv = table("tab_inv", HEADS, NP)
        den = Q[:, :, :].rearrange("p b f -> p (b f)")[:, 0:HEADS * NP // P]

        loaded = sem("loaded")
        loaded_dst = sem("loaded_dst")
        iota_ready = sem("iota_ready")
        extremes = sem("extremes")
        extremes_all = sem("extremes_all")
        spread_w = sem("spread_w")
        stored = sem("stored")
        node = Count(sem("node"))
        var_ready = sem("var_ready")
        dev_ready = sem("dev_ready")
        marks = {}

        def sems(name, *more):
            p = {k: sem(f"{name}_{k}") for k in
                 ("window_step", "table_ready", "onehot_step", "scattered", "done", "post_ready") + more
                 if not k.endswith("_loaded")}
            for k in ("idx_loaded", "gathered") + tuple(m for m in more if m.endswith("_loaded")):
                p[k] = [sem(f"{name}_{k}{u}") for u in range(U)]
            return p

        prop = [sems(f"prop{k}", "agg_free") for k in range(3)]
        tp = sems("tp", "agg_free", "sh_loaded", "prod_ready", "fold_copied", "folded")
        at = sems("at", "qwin_loaded", "turned", "turned_copied", "query_ready", "score_step",
                  "score_ready", "parts_ready", "parts_turned", "parts_copied", "spread_ready",
                  "peak_ready", "peak_back", "diff_ready", "prob_ready", "msg_ready", "merge_step",
                  "merge_in", "mloc_ready", "merge_relu", "merge_exp", "merged",
                  "ht_ready", "ht_copied", "proj_ready", "proj_copied", "q_stored", "norm_moved")
        cv = sems("cv", "agg_free", "sh_loaded", "feat_loaded", "hidden_ready", "hidden_relu",
                  "weights_ready", "scaled", "source_step", "prod_step", "msg_ready", "ht_ready", "ht_copied")

        def dram_nodes(dram):
            return dram[0:NP, :].rearrange("(p b) f -> p (b f)", p=P)

        def flat(tile):
            return tile[:, :, :].rearrange("p b f -> p (b f)")

        def blocks_of(c):
            return min(4, NB - 4 * c)

        NQ = -(-NB // 4)
        WSTEPS = 3

        loads = [
            (flat(X), dram_nodes(t["x"])),
            (ident[:, :], t["c_ident"]), (cg[:, :, :, :], t["c_cg"]), (sel8[:, :], t["c_sel"]),
            (si_mask[:, :, :], t["c_si"]), (feat[0:3 * HEADS, 0, 0:4 * W], t["c_pick"]),
            (w_l1[:, :, :], t["L1_gnn_W"].rearrange("k i o -> i k o")),
            (w_qkv[:, 0, :], t["L2_gnn_Wq"]), (w_qkv[:, 1, :], t["L2_gnn_Wk"]),
            (w_qkv[:, 2, :], t["L2_gnn_Wv"]), (w_o[:, :], t["L2_gnn_Wo"]),
            (w1[:, :], t["L3_gnn_W1"]), (b1[:, :], t["L3_gnn_b1"].rearrange("(m a) -> m a", a=1)),
            *((w2[0:MLP, 64 * k:64 * k + 64], t["L3_gnn_W2"][:, 64 * m:64 * m + 64])
              for k, m in enumerate((3, 1, 0, 2))),
            *((w2[MLP:MLP + 1, 64 * k:64 * k + 64],
               t["L3_gnn_b2"][64 * m:64 * m + 64].rearrange("(a m) -> a m", a=1))
              for k, m in enumerate((3, 1, 0, 2))),
            (si[:, 0, :], t["L3_gnn_si_w0"]), (si[:, 1, :], t["L3_gnn_si_w1"]),
        ]

        block = ctx.enter_context(nc.Block())

        @block.vector
        def _(dve):
            V = nc.vector

            def step(ins):
                node.inc(ins)

            def settle():
                dve.wait_ge(node.sem, node.n)

            def do(ins):
                step(ins)
                settle()

            dve.wait_ge(loaded_dst, 16)
            do(V.tensor_copy(dst[:, :, :], rel[:, :, :].bitcast(I32)))
            do(V.tensor_reduce(base[:, :], dst[:, :, :], AX, ALU.min))
            do(V.tensor_scalar(rel[:, :, :], dst[:, :, :], float(N - 1), None, ALU.min))
            do(V.tensor_reduce(span[:, :], rel[:, :, :], AX, ALU.max))
            V.tensor_scalar(base[:, :], base[:, :], -1.0, None, ALU.mult).then_inc(extremes, 1)
            dve.wait_ge(extremes_all, 2)
            do(V.tensor_scalar(base[:, :], base[:, :], -1.0, None, ALU.mult))
            do(V.tensor_tensor(span[:, :], span[:, :], base[:, :], ALU.subtract))
            do(V.tensor_reduce(reach[:, 0:1], span[:, :], AX, ALU.max))
            dve.wait_ge(iota_ready, 1)
            do(V.tensor_scalar(masked[:, 0:P], iota[:, :], float(W), reach[:, 0:1], ALU.mult, ALU.is_le))
            do(V.tensor_scalar(reach[:, 0:1], reach[:, 0:1], -float(P * W), None, ALU.add))
            do(V.tensor_scalar(masked[:, P:2 * P], iota[:, :], float(W), reach[:, 0:1], ALU.mult, ALU.is_le))
            do(V.tensor_reduce(reach[:, 1:2], masked[:, :], AX, ALU.add))
            do(V.tensor_copy(n_sweeps_i[:, :], reach[:, 1:2]))
            marks["n_sweeps"] = node.n
            n_sweeps = dve.value_load(n_sweeps_i[0:1, 0:1], min_val=1, max_val=NP // W)

            dve.wait_ge(loaded, 16 * len(loads))
            dve.wait_ge(spread_w, 1)
            for mix, (w_rows, r, k, bank) in enumerate(((w_exp, 96, 6, 0), (si_exp, D, 2, 1))):
                got = psum[0:r, bank, 0:8 * k].rearrange("r (k o) -> r k o", k=k)
                step(V.tensor_copy(w_rows[:, :, 0:8], got))
                for m in range(3):
                    step(V.tensor_copy(w_rows[:, :, 8 + m:D:3], got))
            settle()
            for c in range(3):
                step(V.tensor_tensor(cg[:, c, :, :], cg[:, c, :, :], w_exp[:, :, :], ALU.mult))
            step(V.tensor_tensor(si_mask[:, :, :], si_mask[:, :, :], si_exp[:, :, :], ALU.mult))
            settle()
            for c in range(3):
                step(V.tensor_reduce(w_fold[:, c, :], cg[:, c, :, :].rearrange("r i o -> r o i"), AX, ALU.add))
            step(V.tensor_reduce(si_w[:, :], si_mask[:, :, :].rearrange("r i o -> r o i"), AX, ALU.add))
            step(V.tensor_scalar(alpha_i[:, :], ident[0:D, 0:D], ALPHA, None, ALU.mult))
            step(V.tensor_scalar(w2[:, 0:64], w2[:, 0:64], C110, None, ALU.mult))
            step(V.memset(one[:, :], 1.0))
            step(V.tensor_copy(pick[:, :, :].rearrange("r h n -> r (h n)"), feat[0:3 * HEADS, 0, 0:4 * W]))
            step(V.tensor_tensor(both[:, :], ident[:, 0:W], ident[:, W:2 * W], ALU.add))
            step(V.memset(mrep[:, :, :], 0.0))
            step(V.tensor_copy(ident16[:, :], ident[:, :]))
            step(V.memset(rows[:, :, :, D:D + 1], 1.0))

            def bnf(x):
                return x.unsqueeze(2).to_broadcast([P, NB, D])

            def layernorm(k):
                do(V.tensor_reduce(stat[:, 0, :], X[:, :, :], AX, ALU.add))
                do(V.tensor_scalar(stat[:, 0, :], stat[:, 0, :], 1.0 / D, None, ALU.mult))
                do(V.tensor_tensor(C, X[:, :, :], bnf(stat[:, 0, :]), ALU.subtract))
                do(V.tensor_tensor(Q[:, :, :], C, C, ALU.mult))
                do(V.tensor_reduce(stat[:, 1, :], Q[:, :, :], AX, ALU.add))
                V.tensor_scalar(stat[:, 1, :], stat[:, 1, :], 1.0 / D, EPS, ALU.mult,
                                ALU.add).then_inc(var_ready, 1)
                dve.wait_ge(dev_ready, k + 1)
                do(V.reciprocal(stat[:, 0, :], stat[:, 2, :]))
                do(V.tensor_tensor(C, C, bnf(stat[:, 0, :]), ALU.mult))
                do(V.tensor_scalar(H[:, :, :], C, 0.0, None, ALU.max))

            def open_windows(p, w):
                V.tensor_scalar(start[:, :], start[:, :], float(W), None, ALU.add).then_inc(p["window_step"], 1)
                dve.wait_ge(p["window_step"], w * WSTEPS + 1)
                V.tensor_tensor(rel[:, :, :], start[:, :].unsqueeze(2).to_broadcast([P, S, T]), dst[:, :, :],
                                ALU.subtract).then_inc(p["window_step"], 1)
                V.tensor_scalar(off[:, :], start[:, :], float(NP), None, ALU.min).then_inc(p["window_step"], 1)
                dve.wait_ge(p["window_step"], (w + 1) * WSTEPS)
                dve.nop(nofuse=True)

            def before_pass(n):
                step(V.tensor_scalar(start[:, :], base[:, :], -float(W), None, ALU.add))
                do(V.memset(acc[0:n, :], 0.0))

            def windowed(p, turn):
                with dve.Fori(0, n_sweeps) as w:
                    open_windows(p, w)
                    turn((w * NI, 0), None)
                    with dve.Fori(1, NI) as it:
                        turn((w * NI + it, it), (w * NI + it - 1, it - 1))
                    turn(None, (w * NI + NI - 1, NI - 1))
                V.drain().then_inc(p["done"], 1)

            def window_column(it, u):
                return dve.value_load(off[0:1, bass.ds(it * U + u, 1)], min_val=0, max_val=NP)

            def window_columns(turn):
                _, columns = nc.values_load_multi_w_load_instructions(
                    off[0:1, bass.ds(turn[1] * U, U)], engines=[mybir.EngineType.DVE], min_val=0, max_val=NP)
                return columns

            def add_window(p, k, source, credit, bank, itg, it, u):
                g = number(itg, u)
                window = acc[0:k, bass.ds(window_column(it, u), W)]
                dve.wait_ge(p[source], g + 1 + credit)
                dve.wait_ge(p["agg_free"], g + 2)
                V.tensor_tensor(window, window, psum[0:k, bank + u % 2, 0:W],
                                ALU.add).then_inc(p["agg_free"], 1)

            layernorm(0)
            step(V.tensor_copy(Q[:, :, :], H[:, :, :]))
            for k in range(3):
                p = prop[k]
                settle()
                marks[f"prop{k}"] = node.n
                before_pass(D + 1)
                dve.sem_inc(p["agg_free"], 2)

                def turn(here, before):
                    for u in range(U):
                        if a := back(here, before, u, 1):
                            add_window(p, D + 1, "scattered", U, 0, *a)
                windowed(p, turn)
                dve.wait_ge(p["table_ready"], 16)
                for c in range(NC):
                    dve.wait_ge(p["post_ready"], c + 1)
                    blk = slice(c * BPC, (c + 1) * BPC)
                    got = psum[:, c, 0:BPC * (D + 1)].rearrange("p (b k) -> p b k", b=BPC)
                    if k == 0:
                        do(V.tensor_scalar(stat[:, 3, blk], got[:, :, D], 1.0, None, ALU.max))
                        do(V.reciprocal(stat[:, 3, blk], stat[:, 3, blk]))
                    step(V.tensor_tensor(H[:, blk, :], got[:, :, 0:D],
                                         stat[:, 3, blk].unsqueeze(2).to_broadcast([P, BPC, D]), ALU.mult))
                settle()
                step(V.tensor_tensor(Q[:, :, :], Q[:, :, :], H[:, :, :], ALU.add))
            settle()
            do(V.scalar_tensor_tensor(X[:, :, :], Q[:, :, :], 0.25, X[:, :, :], ALU.mult, ALU.add))

            layernorm(1)
            marks["tp"] = node.n
            before_pass(D)
            dve.sem_inc(tp["agg_free"], 2)
            dve.sem_inc(tp["prod_ready"], U)

            def multiply(itg, it, u):
                g = number(itg, u)
                dve.wait_ge(tp["gathered"][u], (itg + 1) * 16 * T)
                dve.wait_ge(tp["sh_loaded"][u], (itg + 1) * 16)
                dve.wait_ge(tp["scattered"], g - 1 + U)
                V.tensor_tensor(prod[:, u % 2, :, :].rearrange("p t (j f) -> p t j f", j=SHK),
                                rows[:, u, :, 0:D].unsqueeze(2).to_broadcast([P, T, SHK, D]),
                                sh[:, u, :, :].unsqueeze(3).to_broadcast([P, T, SHK, D]),
                                ALU.mult).then_inc(tp["prod_ready"], 1)

            def tp_turn(here, before):
                for u in range(U):
                    if a := back(here, before, u, 0):
                        multiply(*a)
                    if a := back(here, before, u, 3):
                        add_window(tp, D, "folded", 2, 2, *a)
            windowed(tp, tp_turn)
            for c in range(NC):
                dve.wait_ge(tp["post_ready"], c + 1)
                blk = slice(c * BPC, (c + 1) * BPC)
                step(V.tensor_tensor(X[:, blk, :], X[:, blk, :],
                                     psum[:, c, 0:BPC * D].rearrange("p (b k) -> p b k", b=BPC), ALU.add))
            settle()

            dve.wait_ge(tp["table_ready"], 16)
            layernorm(2)
            marks["at_rows"] = node.n
            step(V.memset(rows[0:W, 0, 0, 0:2 * D], 0.0))
            settle()
            marks["q_zero"] = node.n
            for c in range(NQ):
                n = blocks_of(c)
                dve.wait_ge(at["proj_ready"], c + 1)
                got = psum[:, 2 + c % 2, 0:96 * n].rearrange("p (b k) -> p b k", b=n)
                V.tensor_scalar(Q[:, 4 * c:4 * c + n, :], got[:, :, 0:D], DH ** -0.5, None, ALU.mult)
                V.tensor_copy(kv_rows[:, 4 * c:4 * c + n, :], got[:, :, D:96]).then_inc(at["proj_copied"], 1)
                blk = slice(4 * c, 4 * c + n)
                step(V.tensor_tensor(X[:, blk, :], X[:, blk, :], H[:, blk, :], ALU.add))
                step(V.memset(acc[0:64, blk.start * P:NACC if c == NQ - 1 else blk.stop * P], 0.0))
            dve.wait_ge(at["proj_copied"], NQ)
            do(V.tensor_copy(Q16[:, :, 0:D], Q[:, :, :]))
            do(V.tensor_tensor(Q[:, :, :], Q[:, :, :], Q16[:, :, 0:D], ALU.subtract))
            do(V.tensor_copy(Q16[:, :, 2 * D:3 * D], Q[:, :, :]))
            do(V.tensor_tensor(Q16[:, :, D:2 * D], Q[:, :, :], Q16[:, :, 2 * D:3 * D], ALU.subtract))
            marks["q_split"] = node.n
            step(V.tensor_scalar(start[:, :], base[:, :], -float(W), None, ALU.add))
            dve.wait_ge(at["table_ready"], 16)
            dve.wait_ge(at["q_stored"], 32)
            do(V.memset(peak[0:64, :], FLOOR))
            for k, r in (("score_ready", 2), ("peak_ready", 1), ("diff_ready", 1), ("msg_ready", U),
                         ("merge_step", 1), ("merge_in", 1), ("merged", 1), ("parts_ready", 2)):
                dve.sem_inc(at[k], r)

            def part(u, k):
                return parts[:, u % 2, :, k * HEADS:(k + 1) * HEADS]

            def at_peak(itg, it, u):
                g = number(itg, u)
                dve.wait_ge(at["spread_ready"], g + 2)
                dve.wait_ge(at["turned_copied"], g + 2)
                dve.nop(nofuse=True)
                for k in range(2):
                    ins = V.tensor_tensor_reduce(psum[:, 1 + k, 0:ST], psum[:, 1 + k, 0:ST], pen[:, u, :], 1.0, FLOOR,
                                                 ALU.add, ALU.max, mloc[:, u % 2, k:k + 1])
                ins.then_inc(at["mloc_ready"], 1)

            def at_peak_rows(itg, it, u):
                g = number(itg, u)
                dve.wait_ge(at["mloc_ready"], g + 1)
                dve.wait_ge(at["scattered"], g - 1 + U)
                for r in range(2):
                    half = slice(r * W, (r + 1) * W)
                    ins = V.tensor_copy(
                        mrep[half, u % 2, :].rearrange("p (c k r d) -> p c k r d", c=2, k=2, r=2)[:, :, :, r, :],
                        mloc[half, u % 2, :].unsqueeze(1).unsqueeze(3).to_broadcast([W, 2, 2, DH]))
                ins.then_inc(at["peak_ready"], 1)

            def at_products(itg, it, u):
                g = number(itg, u)
                dve.wait_ge(at["query_ready"], g + 1)
                dve.wait_ge(at["gathered"][u], (itg + 1) * 16 * T)
                V.tensor_tensor(qk[:, :, :], psum[:, 4 + u % 2, 0:T * D].rearrange("p (t f) -> p t f", t=T),
                                rows[:, u, :, 0:D], ALU.mult).then_inc(at["score_step"], 1)

            def at_score(itg, it, u):
                g = number(itg, u)
                dve.wait_ge(at["score_step"], g * 4 + 1)
                V.tensor_reduce(score[:, u, :, :].rearrange("p t h -> p (t h)"),
                                qk[:, :, :].rearrange("p t (h d) -> p (t h) d", h=HEADS),
                                AX, ALU.add).then_inc(at["score_ready"], 1)

            def at_part0(itg, it, u):
                g = number(itg, u)
                dve.wait_ge(at["score_ready"], g + 3)
                V.tensor_copy(part(u, 0), score[:, u, :, :]).then_inc(at["score_step"], 1)

            def at_rest(itg, it, u):
                g = number(itg, u)
                dve.wait_ge(at["score_step"], g * 4 + 2)
                V.tensor_tensor(rest[:, :, :], score[:, u, :, :], part(u, 0), ALU.subtract
                                ).then_inc(at["score_step"], 1)

            def at_part1(itg, it, u):
                g = number(itg, u)
                dve.wait_ge(at["score_step"], g * 4 + 3)
                V.tensor_copy(part(u, 1), rest[:, :, :]).then_inc(at["score_step"], 1)

            def at_part2(itg, it, u):
                g = number(itg, u)
                dve.wait_ge(at["score_step"], g * 4 + 4)
                V.tensor_tensor(part(u, 2), rest[:, :, :], part(u, 1), ALU.subtract).then_inc(at["parts_ready"], 1)

            def at_shift(itg, it, u):
                g = number(itg, u)
                dve.wait_ge(at["peak_back"], g + 1)
                V.tensor_tensor(diff[:, u, :, :].rearrange("p t h -> p (t h)"),
                                score[:, u, :, :].rearrange("p t h -> p (t h)"),
                                psum[:, 6, 0:T * HEADS], ALU.subtract).then_inc(at["diff_ready"], 1)

            def at_message(itg, it, u):
                g = number(itg, u)
                dve.wait_ge(at["prob_ready"], g + 1)
                V.tensor_tensor(msg[:, u, :, 0:D], rows[:, u, :, D:2 * D], msg[:, u, :, D:2 * D],
                                ALU.mult).then_inc(at["msg_ready"], 1)

            def at_merge_diff(itg, it, u, col):
                g = number(itg, u)
                dve.wait_ge(at["scattered"], g + 1 + U)
                dve.wait_ge(at["merge_in"], g + 1)
                V.tensor_tensor(mdiff[:, :], peak[0:64, bass.ds(col, W)], psum[0:64, 7, W:2 * W],
                                ALU.subtract).then_inc(at["merge_step"], 1)

            def at_merge_peaks(itg, it, u, col):
                g = number(itg, u)
                running = peak[0:64, bass.ds(col, W)]
                dve.wait_ge(at["merge_step"], g * 3 + 2)
                V.tensor_tensor(running, running, psum[0:64, 7, W:2 * W], ALU.max).then_inc(at["merge_in"], 1)

            def at_merge_sums(itg, it, u, col):
                g = number(itg, u)
                dve.wait_ge(at["merge_exp"], g + 1)
                dve.wait_ge(at["merged"], g + 1)
                V.tensor_tensor(merge[:, 0, :], acc[0:64, bass.ds(col, W)], mexp[:, 0, :],
                                ALU.mult).then_inc(at["merge_step"], 1)
                V.tensor_tensor(merge[:, 1, :], psum[0:64, 7, 0:W], mexp[:, 1, :],
                                ALU.mult).then_inc(at["merge_step"], 1)

            def at_merge(itg, it, u, col):
                g = number(itg, u)
                dve.wait_ge(at["merge_step"], g * 3 + 4)
                V.tensor_tensor(acc[0:64, bass.ds(col, W)], merge[:, 0, :], merge[:, 1, :],
                                ALU.add).then_inc(at["merged"], 1)

            def at_turn(here, before):
                if before:
                    columns = window_columns(before)
                for u in range(U):
                    second, third, fourth = (back(here, before, u, k) for k in (2, 3, 4))
                    if third:
                        at_peak(*third)
                    if second:
                        at_products(*second)
                    if third:
                        at_peak_rows(*third)
                    if second:
                        at_score(*second)
                    if fourth:
                        at_merge_diff(*fourth, columns[u])
                    if second:
                        at_part0(*second)
                    if fourth:
                        at_merge_peaks(*fourth, columns[u])
                    if second:
                        at_rest(*second)
                        at_part1(*second)
                        at_part2(*second)
                    if fourth:
                        at_merge_sums(*fourth, columns[u])
                    if third:
                        at_shift(*third)
                    if fourth:
                        at_merge(*fourth, columns[u])
                    if third:
                        at_message(*third)
            windowed(at, at_turn)
            dve.wait_ge(at["done"], 1)
            dve.wait_ge(at["norm_moved"], 32)
            do(V.tensor_scalar(den[:, :], den[:, :], 1e-16, None, ALU.max))
            do(V.reciprocal(den[:, :], den[:, :]))
            marks["inverse"] = node.n
            dve.wait_ge(at["norm_moved"], 48 + 16 * DH)
            do(V.tensor_tensor(acc[0:D, 0:NP], acc[0:D, 0:NP], peak[0:D, 0:NP], ALU.mult))
            marks["at_normal"] = node.n
            for c in range(NC):
                dve.wait_ge(at["post_ready"], c + 1)
                blk = slice(c * BPC, (c + 1) * BPC)
                step(V.tensor_tensor(X[:, blk, :], X[:, blk, :],
                                     psum[:, c, 0:BPC * D].rearrange("p (b k) -> p b k", b=BPC), ALU.add))
            settle()

            layernorm(3)
            do(V.memset(hidden[MLP:MLP + 1, :, :], 1.0))
            marks["cv"] = node.n
            before_pass(D)
            for k, r in (("agg_free", 2), ("msg_ready", U), ("source_step", 1)):
                dve.sem_inc(cv[k], r)

            def cv_source(itg, it, u):
                g = number(itg, u)
                dve.wait_ge(cv["gathered"][u], (itg + 1) * 16 * T)
                dve.wait_ge(cv["sh_loaded"][u], (itg + 1) * 16)
                dve.wait_ge(cv["source_step"], g * 2 + 1)
                V.tensor_tensor(src_t[:, :, :].rearrange("p t (i m) -> p t i m", m=3),
                                rows[:, u, :, DH:D].rearrange("p t (i m) -> p t i m", m=3),
                                sh[:, u, :, 1:4].unsqueeze(2).to_broadcast([P, T, DH, 3]),
                                ALU.mult).then_inc(cv["source_step"], 1)

            def cv_source_dots(itg, it, u):
                g = number(itg, u)
                dve.wait_ge(cv["source_step"], g * 2 + 2)
                V.tensor_reduce(source[:, u, :, 0:DH], src_t[:, :, :].rearrange("p t (i m) -> p t i m", m=3),
                                AX, ALU.add).then_inc(cv["source_step"], 1)

            products = peak[:, PROD0:PROD0 + T * 384].rearrange("p (t k) -> p t k", t=T)

            def cv_products(itg, it, u):
                g = number(itg, u)
                dve.wait_ge(cv["weights_ready"], g + 3)
                dve.wait_ge(cv["source_step"], g * 2 + 3)
                dve.wait_ge(cv["msg_ready"], g + U)
                w = psum[:, 1 + 2 * (u % 2):3 + 2 * (u % 2), :].rearrange("p a (t k) -> p (a t) k", t=2)[:, 0:T, :]
                dve.wait_ge(cv["scaled"], g + 1)
                V.tensor_tensor(
                    products[:, :, 0:192].rearrange("p t (i o) -> p t i o", o=DH),
                    w[:, :, 0:192].rearrange("p t (i o) -> p t i o", o=DH),
                    source[:, u, :, 0:24].unsqueeze(3).to_broadcast([P, T, 24, DH]), ALU.mult)
                for m in range(3):
                    ins = V.tensor_tensor(
                        products[:, :, 192 + 64 * m:256 + 64 * m].rearrange("p t (i o) -> p t i o", o=DH),
                        w[:, :, 192:256].rearrange("p t (i o) -> p t i o", o=DH),
                        source[:, u, :, 24 + m:48:3].unsqueeze(3).to_broadcast([P, T, DH, DH]), ALU.mult)
                ins.then_inc(cv["prod_step"], 1)

            def cv_sums(itg, it, u):
                dve.wait_ge(cv["prod_step"], number(itg, u) * 3 + 1)
                V.tensor_reduce(red[:, :, :], products.rearrange("p t (g i o) -> p (t g) o i", g=6, o=DH),
                                AX, ALU.add).then_inc(cv["prod_step"], 1)

            sums = red[:, :, :].rearrange("p (t g) o -> p t g o", g=6)

            def cv_scale(itg, it, u):
                dve.wait_ge(cv["prod_step"], number(itg, u) * 3 + 2)
                V.tensor_tensor(vec[:, :, :, :], sums[:, :, 1, :].unsqueeze(3).to_broadcast([P, T, DH, 3]),
                                sh[:, u, :, 1:4].unsqueeze(2).to_broadcast([P, T, DH, 3]),
                                ALU.mult).then_inc(cv["prod_step"], 1)
                V.tensor_tensor(msg[:, u, :, 0:DH], sums[:, :, 0, :], sums[:, :, 2, :], ALU.add)

            def cv_message(itg, it, u):
                dve.wait_ge(cv["prod_step"], number(itg, u) * 3 + 3)
                V.tensor_tensor(msg[:, u, :, DH:D].rearrange("p t (o m) -> p t o m", m=3), vec[:, :, :, :],
                                sums[:, :, 3:6, :].rearrange("p t m o -> p t o m"),
                                ALU.add).then_inc(cv["msg_ready"], 1)

            def cv_turn(here, before):
                for u in range(U):
                    now, last, fourth = (back(here, before, u, k) for k in (0, 1, 4))
                    if last:
                        cv_products(*last)
                    if now:
                        cv_source(*now)
                    if last:
                        cv_sums(*last)
                    if now:
                        cv_source_dots(*now)
                    if last:
                        cv_scale(*last)
                    if fourth:
                        add_window(cv, D, "scattered", U, 5, *fourth)
                    if last:
                        cv_message(*last)
            windowed(cv, cv_turn)
            for c in range(NQ):
                n = blocks_of(c)
                dve.wait_ge(cv["post_ready"], c + 1)
                step(V.tensor_tensor(X[:, 4 * c:4 * c + n, :], X[:, 4 * c:4 * c + n, :],
                                     psum[:, 2 + c % 2, 0:n * D].rearrange("p (b k) -> p b k", b=n), ALU.add))
                marks[f"out{c}"] = node.n
            settle()
            marks["out"] = node.n

        @block.sync
        def _(sp):
            sp.dma_start(rel[:, :, :].bitcast(I32), t["dst"]).then_inc(loaded_dst, 16)
            for out_ap, in_ap in loads:
                sp.dma_start(out_ap, in_ap).then_inc(loaded, 16)
            sp.wait_ge(node.sem, marks["n_sweeps"])
            n_sweeps = sp.value_load(n_sweeps_i[0:1, 0:1], min_val=1, max_val=NP // W)

            def load_idx(p, slot_free, itg, it, u):
                sp.wait_ge(p[slot_free], number(itg, u) + 1)
                sp.dma_start(idx[:, u, :], t["src"][bass.ds(it * U + u, 1)].rearrange("a p t -> (a p) t")
                             ).then_inc(p["idx_loaded"][u], 16)

            def every_supertile(load):
                with sp.Fori(0, n_sweeps) as w:
                    with sp.Fori(0, NI) as it:
                        for u in range(U):
                            load(w * NI + it, it, u)

            for k in range(3):
                sp.wait_ge(node.sem, marks[f"prop{k}"])
                sp.dma_start(dram_nodes(tab[k]), flat(H)).then_inc(prop[k]["table_ready"], 16)
                every_supertile(lambda *a: load_idx(prop[k], "scattered", *a))

            sp.wait_ge(node.sem, marks["tp"])
            sp.dma_start(dram_nodes(tab_tp), flat(H)).then_inc(tp["table_ready"], 16)

            def tp_load(itg, it, u):
                load_idx(tp, "prod_ready", itg, it, u)
                sp.dma_start(sh[:, u, :, :], t["sh"][bass.ds(it * U + u, 1)].rearrange("a p t k -> (a p) t k")
                             ).then_inc(tp["sh_loaded"][u], 16)
            every_supertile(tp_load)

            sp.wait_ge(node.sem, marks["q_zero"])
            sp.dma_start(tab_q[NP:NACC, :], rows[0:W, 0, 0, 0:3 * D // 2].bitcast(BF16)).then_inc(at["q_stored"], 16)
            sp.wait_ge(at["proj_copied"], NQ)
            sp.dma_start(dram_nodes(tab_kv), flat(kv_rows)).then_inc(at["table_ready"], 16)
            sp.wait_ge(node.sem, marks["q_split"])
            sp.dma_start(dram_nodes(tab_q), flat(Q16)).then_inc(at["q_stored"], 16)
            sp.wait_ge(at["q_stored"], 32)
            with sp.Fori(0, n_sweeps) as w:
                sp.wait_ge(at["window_step"], (w + 1) * WSTEPS)
                sp.nop(nofuse=True)
                with sp.Fori(0, NI) as it:
                    for u in range(U):
                        load_idx(at, "msg_ready", w * NI + it, it, u)
                        col = sp.value_load(off[0:1, bass.ds(it * U + u, 1)], min_val=0, max_val=NP)
                        for half, parts_of_q in ((slice(0, W), slice(0, 2 * D)), (slice(W, 2 * W), slice(2 * D, 3 * D))):
                            width = parts_of_q.stop - parts_of_q.start
                            sp.dma_start(qwin[half, u, 0:width], tab_q[bass.ds(col, W), parts_of_q]
                                         ).then_inc(at["qwin_loaded"][u], 16)

            sp.wait_ge(at["done"], 1)
            sp.dma_start(tab_den[:, :], acc[D:2 * D:DH, 0:NP]).then_inc(at["norm_moved"], 16)
            sp.wait_ge(at["norm_moved"], 16)
            sp.dma_start(den[:, :], tab_den.rearrange("h (c k) -> (h c) k", c=P // HEADS)
                         ).then_inc(at["norm_moved"], 16)
            sp.wait_ge(node.sem, marks["inverse"])
            sp.dma_start(tab_inv.rearrange("h (c k) -> (h c) k", c=P // HEADS), den[:, :]
                         ).then_inc(at["norm_moved"], 16)
            sp.wait_ge(at["norm_moved"], 48)
            for d in range(DH):
                sp.dma_start(peak[d:D:DH, 0:NP], tab_inv[:, :]).then_inc(at["norm_moved"], 16)

            sp.wait_ge(node.sem, marks["cv"])
            sp.dma_start(dram_nodes(tab_cv), flat(H)).then_inc(cv["table_ready"], 16)

            def cv_load(itg, it, u):
                load_idx(cv, "msg_ready", itg, it, u)
                sp.dma_start(sh[:, u, :, 0:4], t["attr4"][bass.ds(it * U + u, 1)].rearrange("a p t k -> (a p) t k")
                             ).then_inc(cv["sh_loaded"][u], 16)
                sp.dma_start(feat[:, u, :], t["feat"][bass.ds(it * U + u, 1)].rearrange("a f e -> (a f) e")
                             ).then_inc(cv["feat_loaded"][u], 16)
            every_supertile(cv_load)

            sp.wait_ge(node.sem, marks["out"])
            sp.dma_start(dram_nodes(t["out"]), flat(X)).then_inc(stored, 16)
            sp.wait_ge(stored, 16)

        @block.gpsimd
        def _(pool):
            pool.iota(iota[:, :], pattern=[[1, P]], base=0, channel_multiplier=0,
                      allow_small_or_imprecise_dtypes=True).then_inc(iota_ready, 1)
            pool.wait_ge(extremes, 1)
            nc.gpsimd.partition_all_reduce(base[:, :], base[:, :], P, RMAX).then_inc(extremes_all, 1)
            nc.gpsimd.partition_all_reduce(span[:, :], span[:, :], P, RMAX).then_inc(extremes_all, 1)
            pool.wait_ge(node.sem, marks["n_sweeps"])
            n_sweeps = pool.value_load(n_sweeps_i[0:1, 0:1], min_val=1, max_val=NP // W)
            for p, source, width in ((prop[0], tab[0], D), (prop[1], tab[1], D), (prop[2], tab[2], D),
                                     (tp, tab_tp, D), (at, tab_kv, 2 * D), (cv, tab_cv, D)):
                pool.wait_ge(p["table_ready"], 16)
                with pool.Fori(0, n_sweeps) as w:
                    with pool.Fori(0, NI) as it:
                        for u in range(U):
                            pool.wait_ge(p["idx_loaded"][u], (w * NI + it + 1) * 16)
                            pool.nop(nofuse=True)
                            for j in range(T):
                                pool.indirect_dma_start(
                                    rows[:, u, j, 0:width], None, source[:, :],
                                    bass.IndirectOffsetOnAxis(ap=idx[:, u, j:j + 1], axis=0)
                                ).then_inc(p["gathered"][u], 16)

        @block.scalar
        def _(act):
            A = nc.scalar
            act.wait_ge(node.sem, marks["n_sweeps"])
            n_sweeps = act.value_load(n_sweeps_i[0:1, 0:1], min_val=1, max_val=NP // W)

            def act_sweeps(p, turn):
                with act.Fori(0, n_sweeps) as w:
                    act.wait_ge(p["window_step"], (w + 1) * WSTEPS)
                    act.nop(nofuse=True)
                    turn((w * NI, 0), None)
                    with act.Fori(1, NI) as it:
                        turn((w * NI + it, it), (w * NI + it - 1, it - 1))
                    turn(None, (w * NI + NI - 1, NI - 1))

            def make_onehot(p, itg, it, u, copies=1):
                g = number(itg, u)
                act.wait_ge(p["onehot_step"], 2 * g + 1)
                for j in range(T):
                    ins = A.activation(dist[:, j * W:(j + 1) * W], iota[:, 0:W], ACT.Square,
                                       bias=rel[:, bass.ds(it * U + u, 1), j])
                ins.then_inc(p["onehot_step"], 1)
                act.wait_ge(p["onehot_step"], 2 * g + 2)
                act.wait_ge(p["scattered"], g + 1)
                if copies == 1:
                    out, squares = onehot[:, u, :, 0:W], dist[:, :].rearrange("p (t n) -> p t n", t=T)
                else:
                    out = onehot[:, u, :, :].rearrange("p t (c n) -> p t c n", c=2)
                    squares = dist[:, :].rearrange("p (t n) -> p t n", t=T).unsqueeze(2).to_broadcast([P, T, 2, W])
                A.activation(out, squares, ACT.Relu,
                             bias=one[:, 0:1], scale=-1.0).then_inc(p["onehot_step"], 1)

            def deviation(k):
                act.wait_ge(var_ready, k + 1)
                A.activation(stat[:, 2, :], stat[:, 1, :], ACT.Sqrt).then_inc(dev_ready, 1)

            deviation(0)

            for k in range(3):
                act.sem_inc(prop[k]["onehot_step"], 1)

                def prop_turn(here, before):
                    for u in range(U):
                        if a := back(here, before, u, 0):
                            make_onehot(prop[k], *a)
                act_sweeps(prop[k], prop_turn)

            deviation(1)
            act.sem_inc(tp["onehot_step"], 1)

            act.sem_inc(tp["fold_copied"], 2)

            def tp_turn(here, before):
                for u in range(U):
                    if a := back(here, before, u, 0):
                        make_onehot(tp, *a)
                    if a := back(here, before, u, 1):
                        g, slot = number(a[0], a[2]), a[2]
                        act.wait_ge(tp["scattered"], g + 1 + U)
                        act.wait_ge(tp["folded"], g + 1)
                        A.activation(fold_in[:, slot % 2, :], psum[0:96, slot % 2, 0:3 * W],
                                     ACT.Copy).then_inc(tp["fold_copied"], 1)
            act_sweeps(tp, tp_turn)

            deviation(2)

            def copy_turned_rows(p):
                for c in range(NQ):
                    act.wait_ge(p["ht_ready"], c + 1)
                    if c >= 2:
                        act.wait_ge(p["proj_ready" if p is at else "post_ready"], c - 1)
                    A.activation(ht[:, c % 2, 0:blocks_of(c) * P], psum[0:D, c % 2, 0:blocks_of(c) * P],
                                 ACT.Copy).then_inc(p["ht_copied"], 1)

            copy_turned_rows(at)
            for k in ("turned_copied", "parts_copied", "onehot_step"):
                act.sem_inc(at[k], 1)

            def at_turn(here, before):
                for u in range(U):
                    if a := back(here, before, u, 0):
                        make_onehot(at, *a, copies=2)
                    if a := back(here, before, u, 4):
                        g = number(a[0], a[2])
                        act.wait_ge(at["merge_step"], g * 3 + 2)
                        act.wait_ge(at["merged"], g + 1)
                        A.activation(mrelu[:, 0, :], mdiff[:, :], ACT.Relu, scale=-1.0)
                        A.activation(mrelu[:, 1, :], mdiff[:, :], ACT.Relu).then_inc(at["merge_relu"], 1)
                        act.wait_ge(at["merge_relu"], g + 1)
                        A.activation(mexp[:, :, :], mrelu[:, :, :], ACT.Exp, scale=-1.0
                                     ).then_inc(at["merge_exp"], 1)
                    if a := back(here, before, u, 3):
                        g = number(a[0], a[2])
                        act.wait_ge(at["diff_ready"], g + 2)
                        A.activation(msg[:, a[2], :, D:2 * D].rearrange("p t (h d) -> p t h d", h=HEADS),
                                     diff[:, a[2], :, :].unsqueeze(3).to_broadcast([P, T, HEADS, DH]),
                                     ACT.Exp).then_inc(at["prob_ready"], 1)
                    if a := back(here, before, u, 2):
                        g = number(a[0], a[2])
                        act.wait_ge(at["parts_turned"], g + 1)
                        act.wait_ge(at["spread_ready"], g + 1)
                        A.activation(parts_t[:, :], psum16[0:3 * HEADS, 0:ST],
                                     ACT.Copy).then_inc(at["parts_copied"], 1)
                    if a := back(here, before, u, 0):
                        g = number(a[0], a[2])
                        act.wait_ge(at["turned"], g + 1)
                        act.wait_ge(at["msg_ready"], g + 1)
                        A.activation(onehot16[:, a[2] % 2, :], psum[:, 0, 0:ST], ACT.Copy)
                        A.activation(onehot_t[:, a[2], :], psum[:, 0, 0:ST], ACT.Copy)
                        A.activation(pen[:, a[2], :], psum[:, 0, 0:ST], ACT.Copy, bias=-BIG,
                                     scale=BIG).then_inc(at["turned_copied"], 1)
            act_sweeps(at, at_turn)

            deviation(3)

            def cv_turn(here, before):
                for u in range(U):
                    if a := back(here, before, u, 0):
                        g, s = number(a[0], a[2]), a[2]
                        act.wait_ge(cv["hidden_ready"], g + 1)
                        act.wait_ge(cv["weights_ready"], g + 1)
                        A.activation(hidden[0:MLP, s % 2, :], psum[0:MLP, 0, 0:ST], ACT.Relu,
                                     bias=b1[:, 0:1]).then_inc(cv["hidden_relu"], 1)
                        make_onehot(cv, *a)
                        act.wait_ge(cv["gathered"][s], (a[0] + 1) * 16 * T)
                        act.wait_ge(cv["sh_loaded"][s], (a[0] + 1) * 16)
                        A.activation(source[:, s, :, 8:16], rows[:, s, :, 0:DH], ACT.Copy)
                        for j in range(T):
                            ins = A.activation(source[:, s, j, 16:48], rows[:, s, j, 0:D], ACT.Copy,
                                               scale=sh[:, s, j, 0:1])
                        ins.then_inc(cv["scaled"], 1)
            act.sem_inc(cv["hidden_relu"], 1)
            act.sem_inc(cv["onehot_step"], 1)
            act_sweeps(cv, cv_turn)
            copy_turned_rows(cv)

        @block.tensor
        def _(pe):
            M = nc.tensor
            pe.wait_ge(loaded, 16 * len(loads))
            M.matmul(psum[0:96, 0, 0:48], sel8[:, :], w_l1[:, :, :].rearrange("i k o -> i (k o)"),
                     start=True, stop=True)
            M.matmul(psum[0:D, 1, 0:16], sel8[:, 0:D], si[:, :, :].rearrange("i k o -> i (k o)"),
                     start=True, stop=True).then_inc(spread_w, 1)
            pe.wait_ge(node.sem, marks["n_sweeps"])
            n_sweeps = pe.value_load(n_sweeps_i[0:1, 0:1], min_val=1, max_val=NP // W)

            def rows_of_acc(p, k, times):
                for c in range(NC):
                    for j in range(BPC):
                        ins = M.matmul(psum[:, c, j * k:(j + 1) * k], acc[0:k, c * BPC + j:NP:NB],
                                       times, start=True, stop=True)
                    ins.then_inc(p["post_ready"], 1)

            for k in range(3):
                p = prop[k]
                pe.sem_inc(p["scattered"], U)

                def turn(here, before):
                    for u in range(U):
                        if a := back(here, before, u, 0):
                            g = number(a[0], a[2])
                            pe.wait_ge(p["gathered"][u], (a[0] + 1) * 16 * T)
                            pe.wait_ge(p["onehot_step"], 2 * g + 3)
                            pe.wait_ge(p["agg_free"], g + 1)
                            for j in range(T):
                                ins = M.matmul(psum[0:D + 1, u % 2, 0:W], rows[:, u, j, 0:D + 1],
                                               onehot[:, u, j, 0:W], start=(j == 0), stop=(j == T - 1))
                            ins.then_inc(p["scattered"], 1)
                sweeps(pe, n_sweeps, turn)
                pe.wait_ge(p["done"], 1)
                rows_of_acc(p, D + 1, ident[0:D + 1, 0:D + 1])

            pe.sem_inc(tp["scattered"], U)
            pe.sem_inc(tp["folded"], 2)

            def tp_turn(here, before):
                for u in range(U):
                    if a := back(here, before, u, 2):
                        g, s = number(a[0], a[2]), a[2]
                        pe.wait_ge(tp["fold_copied"], g + 3)
                        pe.wait_ge(tp["agg_free"], g + 1)
                        for c in range(3):
                            ins = M.matmul(psum[0:D, 2 + s % 2, 0:W], w_fold[:, c, :],
                                           fold_in[:, s % 2, c * W:(c + 1) * W], start=(c == 0), stop=(c == 2))
                        ins.then_inc(tp["folded"], 1)
                    if a := back(here, before, u, 0):
                        g, s = number(a[0], a[2]), a[2]
                        pe.wait_ge(tp["onehot_step"], 2 * g + 3)
                        pe.wait_ge(tp["prod_ready"], g + 1 + U)
                        pe.wait_ge(tp["fold_copied"], g + 1)
                        for c in range(3):
                            for j in range(T):
                                ins = M.matmul(psum[0:96, s % 2, c * W:(c + 1) * W],
                                               prod[:, s % 2, j, c * 96:(c + 1) * 96],
                                               onehot[:, s, j, 0:W], start=(j == 0), stop=(j == T - 1))
                        ins.then_inc(tp["scattered"], 1)
            sweeps(pe, n_sweeps, tp_turn)
            pe.wait_ge(tp["done"], 1)
            rows_of_acc(tp, D, ident[0:D, 0:D])

            def turn_rows(p, c):
                for j in range(blocks_of(c)):
                    ins = M.transpose(psum[0:D, c % 2, j * P:(j + 1) * P], H[:, 4 * c + j, :], ident[:, :])
                ins.then_inc(p["ht_ready"], 1)

            pe.wait_ge(node.sem, marks["at_rows"])
            for c in range(NQ + 1):
                if c < NQ:
                    if c >= 2:
                        pe.wait_ge(at["ht_copied"], c - 1)
                    turn_rows(at, c)
                if c >= 1:
                    pe.wait_ge(at["ht_copied"], c)
                    if c >= 3:
                        pe.wait_ge(at["proj_copied"], c - 2)
                    for j in range(blocks_of(c - 1)):
                        ins = M.matmul(psum[:, 2 + (c - 1) % 2, j * 96:(j + 1) * 96],
                                       ht[:, (c - 1) % 2, j * P:(j + 1) * P],
                                       w_qkv[:, :, :].rearrange("i k o -> i (k o)"), start=True, stop=True)
                    ins.then_inc(at["proj_ready"], 1)

            pe.sem_inc(at["scattered"], U)
            pe.sem_inc(at["spread_ready"], 1)

            def at_turn(here, before):
                for u in range(U):
                    if a := back(here, before, u, 4):
                        g, s = number(a[0], a[2]), a[2]
                        pe.wait_ge(at["msg_ready"], g + 1 + U)
                        pe.wait_ge(at["merged"], g + 1)
                        for j in range(T):
                            M.matmul(psum[0:64, 7, 0:W], msg[:, s, j, :], onehot[:, s, j, 0:W],
                                           start=(j == 0), stop=(j == T - 1))
                        M.matmul(psum[0:64, 7, W:2 * W], mrep[:, s % 2, :], both[:, :],
                                 start=True, stop=True).then_inc(at["scattered"], 1)
                    if a := back(here, before, u, 1):
                        g, s = number(a[0], a[2]), a[2]
                        pe.wait_ge(at["turned_copied"], g + 2)
                        pe.wait_ge(at["qwin_loaded"][s], (a[0] + 1) * 32)
                        pe.wait_ge(at["score_ready"], g + 1)
                        for j in range(T):
                            M.matmul(psum[:, 4 + s % 2, j * D:(j + 1) * D],
                                     onehot16[:, s % 2, j * P:(j + 1) * P], qwin[:, s, 0:D],
                                     start=True, stop=False)
                            ins = M.matmul(psum[:, 4 + s % 2, j * D:(j + 1) * D],
                                           onehot16[0:W, s % 2, j * P:(j + 1) * P], qwin[0:W, s, D:2 * D],
                                           start=False, stop=True)
                        ins.then_inc(at["query_ready"], 1)
                    if a := back(here, before, u, 3):
                        g, s = number(a[0], a[2]), a[2]
                        pe.wait_ge(at["peak_ready"], g + 2)
                        pe.wait_ge(at["diff_ready"], g + 1)
                        for j in range(T):
                            ins = M.matmul(psum[:, 6, j * HEADS:(j + 1) * HEADS], onehot_t[:, s, j * P:(j + 1) * P],
                                           mrep[:, s % 2, 0:D:DH], start=True, stop=True)
                        ins.then_inc(at["peak_back"], 1)
                    if a := back(here, before, u, 2):
                        g, s = number(a[0], a[2]), a[2]
                        pe.wait_ge(at["parts_ready"], g + 1 + 2)
                        pe.wait_ge(at["parts_copied"], g + 1)
                        for j in range(T):
                            ins = M.transpose(psum16[0:3 * HEADS, j * P:(j + 1) * P], parts[:, s % 2, j, :],
                                              ident16[:, :])
                        ins.then_inc(at["parts_turned"], 1)
                    if a := back(here, before, u, 0):
                        g, s = number(a[0], a[2]), a[2]
                        pe.wait_ge(at["onehot_step"], 2 * g + 3)
                        pe.wait_ge(at["turned_copied"], g + 1)
                        for j in range(T):
                            ins = M.transpose(psum[:, 0, j * P:(j + 1) * P], onehot[:, s, j, :], ident[:, :])
                        ins.then_inc(at["turned"], 1)
                    if a := back(here, before, u, 2):
                        g, s = number(a[0], a[2]), a[2]
                        pe.wait_ge(at["parts_copied"], g + 2)
                        pe.wait_ge(at["peak_ready"], g + 1)
                        for k in range(2):
                            ins = M.matmul(psum[:, 1 + k, 0:ST], pick[:, k, :], parts_t[:, :],
                                           start=True, stop=True)
                        ins.then_inc(at["spread_ready"], 1)
            sweeps(pe, n_sweeps, at_turn)
            pe.wait_ge(node.sem, marks["at_normal"])
            rows_of_acc(at, D, w_o[:, :])

            pe.sem_inc(cv["scattered"], U)
            pe.sem_inc(cv["weights_ready"], 2)

            def cv_turn(here, before):
                for u in range(U):
                    if a := back(here, before, u, 0):
                        g, s = number(a[0], a[2]), a[2]
                        pe.wait_ge(cv["feat_loaded"][s], (a[0] + 1) * 16)
                        pe.wait_ge(cv["hidden_relu"], g + 1)
                        M.matmul(psum[0:MLP, 0, 0:ST], w1[:, :], feat[:, s, :], start=True,
                                 stop=True).then_inc(cv["hidden_ready"], 1)
                    if a := back(here, before, u, 1):
                        g, s = number(a[0], a[2]), a[2]
                        pe.wait_ge(cv["hidden_relu"], g + 2)
                        pe.wait_ge(cv["msg_ready"], g - 1 + U)
                        for j in range(T):
                            ins = M.matmul(psum[:, 1 + 2 * (s % 2) + j // 2, j % 2 * 256:(j % 2 + 1) * 256],
                                           hidden[:, s % 2, j * P:(j + 1) * P], w2[:, :], start=True, stop=True)
                        ins.then_inc(cv["weights_ready"], 1)
                    if a := back(here, before, u, 3):
                        g, s = number(a[0], a[2]), a[2]
                        pe.wait_ge(cv["msg_ready"], g + 1 + U)
                        pe.wait_ge(cv["onehot_step"], 2 * g + 3)
                        pe.wait_ge(cv["agg_free"], g + 1)
                        for j in range(T):
                            ins = M.matmul(psum[0:D, 5 + s % 2, 0:W], msg[:, s, j, 0:D], onehot[:, s, j, 0:W],
                                           start=(j == 0), stop=(j == T - 1))
                        ins.then_inc(cv["scattered"], 1)
            pe.wait_ge(node.sem, marks["cv"])
            sweeps(pe, n_sweeps, cv_turn)
            pe.wait_ge(cv["done"], 1)
            for c in range(NQ + 1):
                if c < NQ:
                    if c >= 2:
                        pe.wait_ge(cv["ht_copied"], c - 1)
                    turn_rows(cv, c)
                if c >= 1:
                    pe.wait_ge(cv["ht_copied"], c)
                    if c >= 3:
                        pe.wait_ge(node.sem, marks[f"out{c - 3}"])
                    for j in range(blocks_of(c - 1)):
                        here = psum[:, 2 + (c - 1) % 2, j * D:(j + 1) * D]
                        M.matmul(here, ht[:, (c - 1) % 2, j * P:(j + 1) * P], si_w[:, :],
                                 start=True, stop=False)
                        ins = M.matmul(here, acc[0:D, 4 * (c - 1) + j:NP:NB], alpha_i[:, :],
                                       start=False, stop=True)
                    ins.then_inc(cv["post_ready"], 1)


def _coupling():
    import math

    def cg_coeff(j1, m1, j2, m2, j3, m3):
        if m3 != m1 + m2:
            return 0.0
        f = math.factorial
        vmin = max(0, j2 - j3 - m1, j1 + m2 - j3)
        vmax = min(j1 + j2 - j3, j1 - m1, j2 + m2)
        pref = (2 * j3 + 1) * f(j3 + j1 - j2) * f(j3 - j1 + j2) * f(j1 + j2 - j3) / f(j1 + j2 + j3 + 1)
        pref *= f(j3 + m3) * f(j3 - m3) * f(j1 - m1) * f(j1 + m1) * f(j2 - m2) * f(j2 + m2)
        s = 0.0
        for v in range(vmin, vmax + 1):
            s += (-1) ** v / (f(v) * f(j1 + j2 - j3 - v) * f(j1 - m1 - v) * f(j2 + m2 - v)
                              * f(j3 - j2 + m1 + v) * f(j3 - j1 - m2 + v))
        return math.sqrt(pref) * s

    def su2(l1, l2, l3):
        c = np.zeros((2 * l1 + 1, 2 * l2 + 1, 2 * l3 + 1), dtype=np.complex128)
        for m1 in range(-l1, l1 + 1):
            for m2 in range(-l2, l2 + 1):
                if -l3 <= m1 + m2 <= l3:
                    c[m1 + l1, m2 + l2, m1 + m2 + l3] = cg_coeff(l1, m1, l2, m2, l3, m1 + m2)
        return c

    def qmat(n):
        q = np.zeros((2 * n + 1, 2 * n + 1), dtype=np.complex128)
        for m in range(-n, 0):
            q[n + m, n + abs(m)] = 1 / np.sqrt(2)
            q[n + m, n - abs(m)] = -1j / np.sqrt(2)
        q[n, n] = 1.0
        for m in range(1, n + 1):
            q[n + m, n + abs(m)] = (-1) ** m / np.sqrt(2)
            q[n + m, n - abs(m)] = 1j * (-1) ** m / np.sqrt(2)
        return (-1j) ** n * q

    cg = np.zeros((96, 3, 6, D), np.float32)
    first = (0, 1, 4)
    for mix, (le, ln, lo) in enumerate(((0, 0, 0), (0, 1, 1), (1, 0, 1), (1, 1, 0), (1, 1, 1), (2, 1, 1))):
        c = np.einsum("ij,kl,mn,ikn->jlm", qmat(le), qmat(ln), np.conj(qmat(lo)).T, su2(le, ln, lo)).real
        c = c / np.linalg.norm(c)
        for a in range(2 * le + 1):
            j = first[le] + a
            for b in range(2 * ln + 1):
                for i in range(8):
                    f = i if ln == 0 else 8 + 3 * i + b
                    for k in range(2 * lo + 1):
                        outs = slice(0, 8) if lo == 0 else slice(8 + k, D, 3)
                        cg[32 * (j % 3) + f, j // 3, mix, outs] = c[a, b, k]
    si = np.zeros((D, 2, D), np.float32)
    si[0:8, 0, 0:8] = 8 ** -0.5
    for m in range(3):
        si[8 + m::3, 1, 8 + m::3] = 8 ** -0.5
    sel = np.zeros((8, 96), np.float32)
    for r in range(96):
        f = r % D
        sel[f if f < 8 else (f - 8) // 3, r] = 1.0
    return cg, si, sel


_WEIGHTS = ["L1_gnn_W", "L2_gnn_Wq", "L2_gnn_Wk", "L2_gnn_Wv", "L2_gnn_Wo", "L3_gnn_W1", "L3_gnn_b1",
            "L3_gnn_W2", "L3_gnn_b2", "L3_gnn_si_w0", "L3_gnn_si_w1"]


def kernel(**inputs):
    import numpy as _np
    import concourse.bacc as _bacc
    from concourse import mybir as _mybir
    from concourse.bass_utils import run_bass_kernel_spmd as _run

    def edges(name, fill=0):
        a = _np.asarray(inputs[name])
        a = a.reshape(a.shape[0], -1)
        a = _np.concatenate([a, _np.full((EP - E, a.shape[1]), fill, a.dtype)])
        return a.reshape(S, P, T, -1)

    x = _np.asarray(inputs["x"])
    cg, si, sel = _coupling()
    arrays = {
        "x": _np.concatenate([x, _np.zeros((NP - N, D), x.dtype)]),
        "src": edges("src")[..., 0],
        "dst": edges("dst", int(NOWHERE))[..., 0].transpose(1, 0, 2),
        "sh": _np.concatenate([edges("edge_weight1"), edges("edge_attr_3"), edges("edge_attr_5")], axis=-1),
        "attr4": edges("edge_attr_4"),
        "feat": edges("edge_attr_32").transpose(0, 3, 2, 1).reshape(S, D, ST),
        "c_ident": _np.eye(P, dtype=_np.float32),
        "c_pick": _np.tile(_np.repeat(_np.eye(HEADS, dtype=_np.float32), W, axis=1), (3, 1)),
        "c_cg": cg, "c_si": si, "c_sel": sel,
    }
    for name in _WEIGHTS:
        arrays[name] = _np.asarray(inputs[name])
    nc = _bacc.Bacc("TRN2", target_bir_lowering=False, num_devices=1)
    t, ins = {}, {}
    for name, a in arrays.items():
        ins[f"in_{name}"] = _np.ascontiguousarray(a)
        t[name] = nc.dram_tensor(f"in_{name}", a.shape, _mybir.dt.from_np(a.dtype), kind="ExternalInput").ap()
    t["out"] = nc.dram_tensor("out_0", (NP, D), F32, kind="ExternalOutput").ap()
    build(nc, t)
    r = _run(nc, [ins], core_ids=[0])
    return r.results[0]["out_0"][0:N]
```
